# Optimizing a Trainium2 kernel written in Bass

```python
import numpy as np
import jax
import jax.numpy as jnp

def _softmax(x, axis=-1):
    return jax.nn.softmax(x, axis=axis)

def _gelu(x):
    return jax.nn.gelu(x, approximate=True)

def _silu(x):
    return jax.nn.silu(x)

def _sigmoid(x):
    return jax.nn.sigmoid(x)

def _layernorm(x, axis=-1, eps=1e-05):
    m = jnp.mean(x, axis=axis, keepdims=True)
    v = jnp.var(x, axis=axis, keepdims=True)
    return (x - m) / jnp.sqrt(v + eps)

def _scatter_add(tgt, idx, src, axis=0):
    return tgt.at[idx].add(src)

def _segment_sum(src, seg, n):
    return jax.ops.segment_sum(src, seg, n)
kernel_name = 'mk_adaln_d1_jaxref_r8_b4ba29'

def setup_inputs(seed: int=0):
    np.random.seed(seed)
    _w = jnp.asarray

    def _L0_attn_setup():
        import jax, jax.numpy as jnp
        import numpy as np
        INPUT_SIZE = 128
        STATE_SIZE = 128
        OUTPUT_SIZE = 128
        key = jax.random.key(seed)
        ks = jax.random.split(key, 8)
        B, T = (8, 256)
        u = jax.random.normal(ks[0], (B, T, INPUT_SIZE), dtype=jnp.float32)
        log_A = jax.random.normal(ks[1], (STATE_SIZE,), dtype=jnp.float32) * 0.5
        sB = 1.0 / np.sqrt(INPUT_SIZE)
        sC = 1.0 / np.sqrt(STATE_SIZE)
        sD = 1.0 / np.sqrt(INPUT_SIZE)
        W_B = jax.random.uniform(ks[2], (STATE_SIZE, INPUT_SIZE), jnp.float32, -sB, sB)
        b_B = jax.random.uniform(ks[3], (STATE_SIZE,), jnp.float32, -sB, sB)
        W_C = jax.random.uniform(ks[4], (OUTPUT_SIZE, STATE_SIZE), jnp.float32, -sC, sC)
        b_C = jax.random.uniform(ks[5], (OUTPUT_SIZE,), jnp.float32, -sC, sC)
        W_D = jax.random.uniform(ks[6], (OUTPUT_SIZE, INPUT_SIZE), jnp.float32, -sD, sD)
        b_D = jax.random.uniform(ks[7], (OUTPUT_SIZE,), jnp.float32, -sD, sD)
        log_dt = jnp.full((1,), -1.0, dtype=jnp.float32)
        return {'u': u, 'log_A': log_A, 'W_B': W_B, 'b_B': b_B, 'W_C': W_C, 'b_C': b_C, 'W_D': W_D, 'b_D': b_D, 'log_dt': log_dt}
    _L0_attn_in = _L0_attn_setup()

    def _L0_ffn_setup():
        import jax, jax.numpy as jnp
        import numpy as np
        NUM_EXPERTS = 160
        TOP_K = 8
        ROUTED_SCALE = 2.5
        HIDDEN = 128
        INTER = 64
        key = jax.random.key(seed)
        ks = jax.random.split(key, 7)
        B, S = (1, 256)
        return {'hidden_states': jax.random.normal(ks[0], (B, S, HIDDEN), dtype=jnp.float32), 'router_w': jax.random.normal(ks[1], (NUM_EXPERTS, HIDDEN), dtype=jnp.float32) * 0.02, 'expert_bias': jnp.zeros((NUM_EXPERTS,), dtype=jnp.float32), 'w_gate': jax.random.normal(ks[2], (NUM_EXPERTS, INTER, HIDDEN), dtype=jnp.float32) * 0.02, 'w_down': jax.random.normal(ks[3], (NUM_EXPERTS, HIDDEN, INTER), dtype=jnp.float32) * 0.02, 'w_gate_shared': jax.random.normal(ks[4], (INTER, HIDDEN), dtype=jnp.float32) * 0.02, 'w_down_shared': jax.random.normal(ks[5], (HIDDEN, INTER), dtype=jnp.float32) * 0.02}
    _L0_ffn_in = _L0_ffn_setup()
    _L0_c = _w((lambda *s: np.random.randn(*s).astype(np.float32) * 0.05)(1, 128))
    _L0_wmod = _w((lambda *s: np.random.randn(*s).astype(np.float32) * 0.05)(128, 6 * 128) * 128 ** (-0.5))
    _d = {'L0_attn_u': _L0_attn_in['u'], 'L0_attn_log_A': _L0_attn_in['log_A'], 'L0_attn_W_B': _L0_attn_in['W_B'], 'L0_attn_b_B': _L0_attn_in['b_B'], 'L0_attn_W_C': _L0_attn_in['W_C'], 'L0_attn_b_C': _L0_attn_in['b_C'], 'L0_attn_W_D': _L0_attn_in['W_D'], 'L0_attn_b_D': _L0_attn_in['b_D'], 'L0_attn_log_dt': _L0_attn_in['log_dt'], 'L0_ffn_router_w': _L0_ffn_in['router_w'], 'L0_ffn_expert_bias': _L0_ffn_in['expert_bias'], 'L0_ffn_w_gate': _L0_ffn_in['w_gate'], 'L0_ffn_w_down': _L0_ffn_in['w_down'], 'L0_ffn_w_gate_shared': _L0_ffn_in['w_gate_shared'], 'L0_ffn_w_down_shared': _L0_ffn_in['w_down_shared'], 'L0_c': _L0_c, 'L0_wmod': _L0_wmod}
    _x0 = _d['L0_attn_u']
    _d['L0_attn_u'] = jax.random.normal(jax.random.fold_in(jax.random.key(seed), 1), (1, 2048, 128), dtype=_x0.dtype)
    del _x0
    return _d

def reference(L0_attn_u, L0_attn_log_A, L0_attn_W_B, L0_attn_b_B, L0_attn_W_C, L0_attn_b_C, L0_attn_W_D, L0_attn_b_D, L0_attn_log_dt, L0_ffn_router_w, L0_ffn_expert_bias, L0_ffn_w_gate, L0_ffn_w_down, L0_ffn_w_gate_shared, L0_ffn_w_down_shared, L0_c, L0_wmod):

    def _L0_attn_ref(u, log_A, W_B, b_B, W_C, b_C, W_D, b_D, log_dt):
        import jax, jax.numpy as jnp
        import numpy as np
        INPUT_SIZE = 128
        STATE_SIZE = 128
        OUTPUT_SIZE = 128
        dt = jnp.exp(log_dt)
        A = -jnp.exp(log_A)
        A_bar = jnp.exp(A * dt)
        Bu = (jnp.einsum('bti,ni->btn', u, W_B) + b_B) * dt
        Bu_t = jnp.swapaxes(Bu, 0, 1)

        def step(x, bu):
            x = A_bar * x + bu
            return (x, x)
        x0 = jnp.zeros((u.shape[0], A_bar.shape[0]), dtype=u.dtype)
        _, xs = jax.lax.scan(step, x0, Bu_t)
        xs = jnp.swapaxes(xs, 0, 1)
        y = jnp.einsum('btn,on->bto', xs, W_C) + b_C + jnp.einsum('bti,oi->bto', u, W_D) + b_D
        return y

    def _L0_ffn_ref(hidden_states, router_w, expert_bias, w_gate, w_down, w_gate_shared, w_down_shared):
        import jax, jax.numpy as jnp
        import numpy as np
        NUM_EXPERTS = 160
        TOP_K = 8
        ROUTED_SCALE = 2.5
        HIDDEN = 128
        INTER = 64
        B, S, H = hidden_states.shape
        x = hidden_states.reshape(-1, H)
        T = x.shape[0]
        logits = x @ router_w.T + expert_bias[None, :]
        probs = jax.nn.sigmoid(logits)
        top_w, top_idx = jax.lax.top_k(probs, TOP_K)
        top_w = top_w / (jnp.sum(top_w, axis=-1, keepdims=True) + 1e-09)
        top_w = top_w * ROUTED_SCALE
        combine = jnp.zeros((T, NUM_EXPERTS), dtype=x.dtype)
        combine = combine.at[jnp.arange(T)[:, None], top_idx].set(top_w)
        h1 = jax.nn.silu(jnp.einsum('th,eih->eti', x, w_gate))
        h1w = h1 * combine.T[:, :, None]
        routed = jnp.einsum('eti,ehi->th', h1w, w_down)
        shared = jax.nn.silu(x @ w_gate_shared.T) @ w_down_shared.T
        return (routed + shared).reshape(B, S, H)
    x = L0_attn_u
    mod = (_silu(L0_c) @ L0_wmod).reshape(L0_c.shape[0], 6, 1, -1)
    sa, ca, ga, sb, cb, gb = (mod[:, 0], mod[:, 1], mod[:, 2], mod[:, 3], mod[:, 4], mod[:, 5])
    ga = (2 * (ga >= 0) - 1) * jnp.maximum(jnp.abs(ga), 0.25)
    gb = (2 * (gb >= 0) - 1) * jnp.maximum(jnp.abs(gb), 0.25)
    h = _layernorm(x, axis=-1) * (1 + ca) + sa
    x = x + ga * _L0_attn_ref(h, L0_attn_log_A, L0_attn_W_B, L0_attn_b_B, L0_attn_W_C, L0_attn_b_C, L0_attn_W_D, L0_attn_b_D, L0_attn_log_dt)
    h = _layernorm(x, axis=-1) * (1 + cb) + sb
    x = x + gb * _L0_ffn_ref(h, L0_ffn_router_w, L0_ffn_expert_bias, L0_ffn_w_gate, L0_ffn_w_down, L0_ffn_w_gate_shared, L0_ffn_w_down_shared)
    return x

_drawn_inputs = setup_inputs


def setup_inputs(seed=0):
    import zlib

    import numpy as np

    out = dict(_drawn_inputs(seed))
    spreads = {'L0_ffn_expert_bias': (0.0, 0.8)}
    factors = {'L0_attn_log_A': 4.41,
     'L0_attn_b_B': 5.246,
     'L0_attn_b_C': 4.003,
     'L0_attn_b_D': 4.275,
     'L0_ffn_router_w': 8.0,
     'L0_ffn_w_gate': 8.0,
     'L0_ffn_w_down': 8.0,
     'L0_ffn_w_gate_shared': 8.0,
     'L0_ffn_w_down_shared': 8.0}
    for name, (base, spread) in spreads.items():
        noise = np.random.default_rng([zlib.crc32(name.encode()), seed]).standard_normal(out[name].shape)
        drawn = base * np.exp(spread * noise) if base else spread * noise
        out[name] = jnp.asarray(drawn.astype(out[name].dtype))
    for name, factor in factors.items():
        out[name] = (out[name] * factor).astype(out[name].dtype)
    return out
```

```python
from contextlib import ExitStack

import concourse.bass as bass
from concourse import mybir

F32 = mybir.dt.float32
F32R = mybir.dt.float32r
ALU = mybir.AluOpType
ACT = mybir.ActivationFunctionType
AX_X = mybir.AxisListType.X

P = 128
T = 2048
H = 128
NE = 160
INTER = 64
TOPK = 8
SCALE = 2.5
LN_EPS = 1e-5
SUM_EPS = 1e-9
GATE_FLOOR = 0.25

BANK = 512
TILES = T // P
GT = BANK // P
GROUPS = T // BANK
CHUNK = 2 * BANK
CHUNKS = T // CHUNK
GC = GROUPS // CHUNKS

EC = NE + 2
PAIRS = EC // 2
WG = 3
WGROUPS = PAIRS // WG
RING = 3
BODY = RING * WG
TURNS = PAIRS // BODY
ALL_PAIRS = CHUNKS * PAIRS
ALL_WGROUPS = CHUNKS * WGROUPS

O_WB, O_WC, O_WD, O_RT = 0, 128, 256, 384
SA, CA, GA, SB, CB, GB = range(6)
M_COL = H
M_ALL = H + 6
O_BC, O_BD, O_EB = 0, 128, 256

assert PAIRS == TURNS * BODY and WGROUPS * WG == PAIRS


def adaln_layer(nc: bass.Bass, x: bass.AP, columns: bass.AP, log_dt: bass.AP, rows: bass.AP,
                wmod: bass.AP, proj: bass.AP, experts: bass.AP, out: bass.AP):
    ctx = ExitStack()
    with ctx:
        def sb(name, shape, dt=F32):
            return ctx.enter_context(nc.sbuf_tensor(name, shape, dt))

        def sem(name):
            return ctx.enter_context(nc.semaphore(name))

        cols_sb = sb("cols_sb", [P, 3])
        logdt_sb = sb("logdt_sb", [P, 1])
        rows_sb = sb("rows_sb", [P, 2 * H + NE])
        wmod_sb = sb("wmod_sb", [P, 6 * H])
        proj_sb = sb("proj_sb", [P, 3 * H + NE])
        ident = sb("ident", [P, P])
        ones = sb("ones", [P, P])
        neg_half = sb("neg_half", [P, GT])
        zeros_r = sb("zeros_r", [P, P], F32R)
        exp_a = sb("exp_a", [P, 1])
        dt_sb = sb("dt_sb", [P, 1])
        a_dt = sb("a_dt", [P, 1])
        a_bar = sb("a_bar", [P, 1])
        dt_bias = sb("dt_bias", [P, 1])
        sig_c = sb("sig_c", [P, 1])
        silu_c = sb("silu_c", [P, 1])
        silu_rep = sb("silu_rep", [P, P])
        mod = sb("mod", [P, M_ALL])
        mod_p1 = sb("mod_p1", [P, M_ALL])
        mod_abs = sb("mod_abs", [P, M_ALL])
        mod_mag = sb("mod_mag", [P, M_ALL])
        mod_sgn = sb("mod_sgn", [P, M_ALL])
        mod_gate = sb("mod_gate", [P, M_ALL])
        wc_g = sb("wc_g", [P, H])
        wd_g = sb("wd_g", [P, H])
        bias_sum = sb("bias_sum", [P, H])
        bias_g = sb("bias_g", [P, H])
        x_sb = sb("x_sb", [P, TILES, H])
        xn = sb("xn", [P, TILES, H])
        bn = sb("bn", [P, 2, TILES, 6])
        mv = sb("mv", [P, 2, TILES, 2])
        ve = sb("ve", [P, 2, TILES])
        rstd = sb("rstd", [P, 2, TILES])
        hT = sb("hT", [P, T])
        buT = sb("buT", [P, T])
        stT = sb("stT", [P, T])
        h2T = sb("h2T", [P, T])
        h2_hi = sb("h2_hi", [P, T], F32R)
        h2_lo = sb("h2_lo", [P, T], F32R)
        probs = sb("probs", [P, TILES, NE])
        rest = sb("rest", [P, TILES, NE])
        top8 = sb("top8", [P, TILES, TOPK])
        top_sum = sb("top_sum", [P, TILES])
        top_sum_e = sb("top_sum_e", [P, TILES])
        top_inv = sb("top_inv", [P, TILES])
        sel = sb("sel", [P, TILES, NE])
        comb = sb("comb", [P, TILES, EC])
        combT_a = sb("combT_a", [P, T])
        combT_b = sb("combT_b", [EC - P, T])
        cb = sb("cb", [P, RING, CHUNK])
        w_raw = sb("w_raw", [P, RING, 2 * WG * P])
        w_hi = sb("w_hi", [P, RING, 2 * WG * P], F32R)
        w_lo = sb("w_lo", [P, RING, 2 * WG * P], F32R)
        g_hi = sb("g_hi", [P, RING, CHUNK], F32R)
        g_lo = sb("g_lo", [P, RING, CHUNK], F32R)
        ffT, out_sb = buT, xn

        comb_dram = nc.dram_tensor("combine_scratch", (CHUNKS, EC, CHUNK), F32, kind="Internal").ap()
        comb_rows = comb_dram.rearrange("c e t -> (c e) t")

        ps = ctx.enter_context(nc.psum_tensor("ps", [P, 8, BANK], F32))
        B_XT, B_H2T, B_BU, B_Y, B_LOGIT, B_CTA, B_CTB = 0, 1, 2, 3, 4, 6, 7
        B_MOD = 7
        B_ACC = 6

        def slot(s):
            return ps[:, 2 * s:2 * s + 2, :]

        cols_loaded = sem("cols_loaded")
        rows_loaded = sem("rows_loaded")
        wmod_loaded = sem("wmod_loaded")
        proj_loaded = sem("proj_loaded")
        x_loaded = [sem(f"x_loaded{g}") for g in range(GROUPS)]
        w_loaded = [sem(f"w_loaded{s}") for s in range(RING)]
        cb_loaded = [sem(f"cb_loaded{s}") for s in range(RING)]
        comb_stored = [sem(f"comb_stored{c}") for c in range(CHUNKS)]
        out_stored = sem("out_stored")
        consts_set = sem("consts_set")
        ident_set = sem("ident_set")
        exps_done = sem("exps_done")
        adt_done = sem("adt_done")
        abar_done = sem("abar_done")
        sigc_done = sem("sigc_done")
        siluc_done = sem("siluc_done")
        mod_product = sem("mod_product")
        mod_read = sem("mod_read")
        mod_ready = sem("mod_ready")
        bias_part = sem("bias_part")
        mixer_weights = sem("mixer_weights")
        bn_done = [sem(f"bn_done{n}") for n in range(2)]
        mv_done = [sem(f"mv_done{n}") for n in range(2)]
        var_ready = [sem(f"var_ready{n}") for n in range(2)]
        rstd_ready = [sem(f"rstd_ready{n}") for n in range(2)]
        xn_ready = [sem(f"xn_ready{n}") for n in range(2)]
        xT_done = [sem(f"xT_done{n}") for n in range(2)]
        hT_ready = sem("hT_ready")
        bu_done = sem("bu_done")
        bu_ready = sem("bu_ready")
        states_ready = sem("states_ready")
        y_done = sem("y_done")
        xbias_ready = sem("xbias_ready")
        x1_ready = sem("x1_ready")
        h2T_ready = sem("h2T_ready")
        h2_hi_ready = sem("h2_hi_ready")
        h2_lo_ready = sem("h2_lo_ready")
        logits_done = sem("logits_done")
        probs_ready = sem("probs_ready")
        top8_done = sem("top8_done")
        rest_ready = sem("rest_ready")
        sum_done = sem("sum_done")
        inv_ready = sem("inv_ready")
        sel_ready = sem("sel_ready")
        comb_ready = sem("comb_ready")
        combT_done = sem("combT_done")
        combT_ready = sem("combT_ready")
        w_hi_done = sem("w_hi_done")
        w_split = sem("w_split")
        z_ready = sem("z_ready")
        silu_done = sem("silu_done")
        gated = sem("gated")
        hi_ready = sem("hi_ready")
        lo_ready = sem("lo_ready")
        down_done = sem("down_done")
        acc_read = sem("acc_read")
        ffn_turned = sem("ffn_turned")
        out_ready = sem("out_ready")

        block = ctx.enter_context(nc.Block())

        def tok(g):
            return slice(g * BANK, (g + 1) * BANK)

        def tiles(g):
            return slice(g * GT, (g + 1) * GT)

        def x_dram(a, g):
            return a[0, tok(g), :].rearrange("(q p) h -> p q h", p=P)

        @block.sync
        def _(sp):
            for g in range(GROUPS):
                sp.dma_start(x_sb[:, tiles(g), :], x_dram(x, g)).then_inc(x_loaded[g], 16)
                if g == 0:
                    sp.dma_start(proj_sb[:, :], proj).then_inc(proj_loaded, 16)

            def load_weights(group, s):
                sp.dma_start(w_raw[:, s, :], experts[bass.ds(group, 1), :, :].rearrange("a p n -> (a p) n")
                             ).then_inc(w_loaded[s], 16)

            def load_combine(pair, s):
                for half in range(2):
                    row = comb_rows[bass.ds(2 * pair + half, 1), :]
                    sp.dma_start(cb[INTER * half:INTER * (half + 1), s, :],
                                 row.to_broadcast((INTER, CHUNK))).then_inc(cb_loaded[s], 16)

            for group in range(RING):
                load_weights(group, group)
            for c in range(CHUNKS):
                sp.wait_ge(combT_ready, GC * (c + 1))
                cols = slice(c * CHUNK, (c + 1) * CHUNK)
                sp.dma_start(comb_dram[c, 0:P, :], combT_a[:, cols]).then_inc(comb_stored[c], 16)
                sp.dma_start(comb_dram[c, P:EC, :], combT_b[:, cols]).then_inc(comb_stored[c], 16)
                if c == 0:
                    sp.wait_ge(comb_stored[0], 32)
                    for pair in range(RING):
                        load_combine(pair, pair)
            sp.wait_ge(comb_stored[1], 32)

            def turn(c, i, last):
                for k in range(BODY):
                    j = PAIRS * c + BODY * i + k
                    if k % WG == 0 and not (last and c == CHUNKS - 1):
                        group = WGROUPS * c + WG * i + k // WG
                        sp.wait_ge(w_split, group + 1)
                        nxt = k // WG if last else WG * i + k // WG + RING
                        load_weights(nxt, k // WG)
                    if not (last and c == CHUNKS - 1 and k + RING >= BODY):
                        sp.wait_ge(gated, j + 1)
                        load_combine(j + RING, k % RING)

            for c in range(CHUNKS):
                with sp.Fori(0, TURNS - 1) as i:
                    turn(c, i, False)
                turn(c, TURNS - 1, True)

            for g in range(GROUPS):
                sp.wait_ge(out_ready, g + 1)
                sp.dma_start(x_dram(out, g), out_sb[:, tiles(g), :]).then_inc(out_stored, 16)
            sp.wait_ge(out_stored, 16 * GROUPS)

        @block.gpsimd
        def _(pool):
            pool.memset(ident[:, :], 0.0).then_inc(consts_set, 1)
            pool.memset(neg_half[:, :], -0.5).then_inc(consts_set, 1)
            pool.memset(ones[:, :], 1.0).then_inc(consts_set, 1)
            pool.memset(zeros_r[:, :].bitcast(F32), 0.0).then_inc(consts_set, 1)
            pool.memset(comb[:, :, NE:NE + 1], 1.0).then_inc(consts_set, 1)
            pool.memset(comb[:, :, NE + 1:EC], 0.0).then_inc(consts_set, 1)
            pool.wait_ge(consts_set, 6)
            pool.affine_select(out=ident[:, :], in_=ident[:, :], compare_op=ALU.not_equal, fill=1.0,
                               base=0, pattern=[[-1, P]], channel_multiplier=1).then_inc(ident_set, 1)

            def inv_std(n, g):
                pool.wait_ge(var_ready[n], g + 1)
                pool.tensor_tensor(rstd[:, n, tiles(g)], ve[:, n, tiles(g)], neg_half[:, :],
                                   ALU.pow).then_inc(rstd_ready[n], 1)

            def add_bias(g):
                if g == 0:
                    pool.wait_ge(mixer_weights, 3)
                pool.wait_ge(xn_ready[0], g + 1)
                pool.tensor_tensor(x_sb[:, tiles(g), :], x_sb[:, tiles(g), :],
                                   bias_g[:, :].rearrange("p (a h) -> p a h", a=1).to_broadcast((P, GT, H)),
                                   ALU.add).then_inc(xbias_ready, 1)

            def input_lo(g):
                pool.wait_ge(h2T_ready, g + 1)
                pool.wait_ge(h2_hi_ready, g + 1)
                pool.tensor_tensor(h2_lo[:, tok(g)], h2T[:, tok(g)], h2_hi[:, tok(g)].bitcast(F32),
                                   ALU.subtract).then_inc(h2_lo_ready, 1)

            def select(g):
                pool.wait_ge(rest_ready, g + 1)
                pool.tensor_tensor(sel[:, tiles(g), :], probs[:, tiles(g), :], rest[:, tiles(g), :],
                                   ALU.subtract).then_inc(sel_ready, 1)

            def split_weights(group, s, use):
                pool.wait_ge(w_loaded[s], 16 * use)
                pool.tensor_tensor(w_hi[:, s, :].rearrange("p (a n) -> p a n", n=P),
                                   w_raw[:, s, :].rearrange("p (a n) -> p a n", n=P),
                                   ones[:, :].rearrange("p (a n) -> p a n", a=1).to_broadcast((P, 2 * WG, P)),
                                   ALU.mult).then_inc(w_hi_done, 1)
                pool.wait_ge(w_hi_done, group + 1)
                pool.tensor_tensor(w_lo[:, s, :], w_raw[:, s, :], w_hi[:, s, :].bitcast(F32),
                                   ALU.subtract).then_inc(w_split, 1)

            for g in range(3):
                inv_std(0, g)
            add_bias(0)
            inv_std(0, 3)
            for g in range(1, GROUPS):
                add_bias(g)
            inv_std(1, 0)
            inv_std(1, 1)
            input_lo(0)
            inv_std(1, 2)
            select(0)
            input_lo(1)
            inv_std(1, 3)
            split_weights(0, 0, 1)
            select(1)
            input_lo(2)
            select(2)
            input_lo(3)
            select(3)
            split_weights(1, 1, 1)
            split_weights(2, 2, 1)

            def turn(c, i, last):
                for s in range(BODY // WG):
                    if last and c == CHUNKS - 1:
                        continue
                    group = WGROUPS * c + WG * i + s
                    pool.wait_ge(down_done, WG * (group + 1))
                    split_weights(group + RING, s, WGROUPS // RING * c + i + 2)

            for c in range(CHUNKS):
                with pool.Fori(0, TURNS - 1) as i:
                    turn(c, i, False)
                turn(c, TURNS - 1, True)

        @block.scalar
        def _(act):
            act.dma_start(cols_sb[:, :], columns).then_inc(cols_loaded, 16)
            act.dma_start(logdt_sb[:, :], log_dt.to_broadcast((P, 1))).then_inc(cols_loaded, 16)
            act.dma_start(wmod_sb[:, :], wmod).then_inc(wmod_loaded, 16)
            act.dma_start(rows_sb[:, :], rows.to_broadcast((P, 2 * H + NE))).then_inc(rows_loaded, 16)
            act.wait_ge(cols_loaded, 32)
            act.activation(exp_a[:, :], cols_sb[:, 1:2], ACT.Exp).then_inc(exps_done, 1)
            act.activation(dt_sb[:, :], logdt_sb[:, :], ACT.Exp).then_inc(exps_done, 1)
            act.wait_ge(adt_done, 1)
            act.activation(a_bar[:, :], a_dt[:, :], ACT.Exp, scale=-1.0).then_inc(abar_done, 1)
            act.activation(sig_c[:, :], cols_sb[:, 0:1], ACT.Sigmoid).then_inc(sigc_done, 1)

            def modulate_1(g):
                if g == 0:
                    act.wait_ge(mod_ready, 1)
                act.wait_ge(xT_done[0], g + 1)
                act.activation(hT[:, tok(g)], ps[:, B_XT, :], ACT.Identity,
                               bias=mod[:, M_COL + SA:M_COL + SA + 1],
                               scale=mod_p1[:, M_COL + CA:M_COL + CA + 1]).then_inc(hT_ready, 1)

            def scale_bu(g):
                act.wait_ge(bu_done, g + 1)
                act.activation(buT[:, tok(g)], ps[:, B_BU, :], ACT.Identity, bias=dt_bias[:, :],
                               scale=dt_sb[:, :]).then_inc(bu_ready, 1)

            def modulate_2(g):
                act.wait_ge(xT_done[1], g + 1)
                for dst, done in ((h2T, h2T_ready), (h2_hi, h2_hi_ready)):
                    act.activation(dst[:, tok(g)], ps[:, B_H2T, :], ACT.Identity,
                                   bias=mod[:, M_COL + SB:M_COL + SB + 1],
                                   scale=mod_p1[:, M_COL + CB:M_COL + CB + 1]).then_inc(done, 1)

            def router_probs(g):
                act.wait_ge(logits_done, g + 1)
                act.activation(probs[:, tiles(g), :].rearrange("p (b q) e -> p b (q e)", b=2),
                               ps[:, B_LOGIT:B_LOGIT + 2, 0:2 * NE], ACT.Sigmoid).then_inc(probs_ready, 1)

            def keep_combT(g):
                act.wait_ge(combT_done, g + 1)
                act.activation(combT_a[:, tok(g)], ps[:, B_CTA, :], ACT.Identity)
                act.activation(combT_b[:, tok(g)], ps[0:EC - P, B_CTB, :], ACT.Identity
                               ).then_inc(combT_ready, 1)

            for stage, g in ((modulate_1, 0), (modulate_1, 1), (scale_bu, 0), (modulate_1, 2),
                             (scale_bu, 1), (modulate_1, 3), (scale_bu, 2), (scale_bu, 3),
                             (modulate_2, 0), (router_probs, 0), (modulate_2, 1), (router_probs, 1),
                             (modulate_2, 2), (router_probs, 2), (keep_combT, 0), (modulate_2, 3),
                             (router_probs, 3), (keep_combT, 1), (keep_combT, 2), (keep_combT, 3)):
                stage(g)

            def silu(j, s):
                act.wait_ge(z_ready, j + 1)
                act.activation(slot(s), slot(s), ACT.Silu).then_inc(silu_done, 1)

            def gated_hi(j, s):
                act.wait_ge(gated, j + 1)
                act.activation(g_hi[:, s, :].rearrange("p (b n) -> p b n", b=2), slot(s), ACT.Identity
                               ).then_inc(hi_ready, 1)

            def turn(c, i, last):
                for k in range(BODY):
                    j = PAIRS * c + BODY * i + k
                    if not (last and c == CHUNKS - 1 and k == BODY - 1):
                        silu(j + 1, (k + 1) % RING)
                    gated_hi(j, k % RING)

            silu(0, 0)
            for c in range(CHUNKS):
                with act.Fori(0, TURNS - 1) as i:
                    turn(c, i, False)
                turn(c, TURNS - 1, True)
                act.wait_ge(down_done, PAIRS * (c + 1))
                act.activation(ffT[:, c * CHUNK:(c + 1) * CHUNK].rearrange("p (b n) -> p b n", b=2),
                               ps[:, B_ACC:B_ACC + 2, :], ACT.Identity,
                               scale=mod_gate[:, M_COL + GB:M_COL + GB + 1]).then_inc(acc_read, 1)

        @block.vector
        def _(dve):
            def ln_stats(n, g):
                if n == 0:
                    dve.wait_ge(x_loaded[g], 16)
                else:
                    dve.wait_ge(x1_ready, g + 1)
                for t in range(g * GT, (g + 1) * GT):
                    last = dve.bn_stats(bn[:, n, t, :], x_sb[:, t, :])
                last.then_inc(bn_done[n], 1)
                dve.wait_ge(bn_done[n], g + 1)
                for t in range(g * GT, (g + 1) * GT):
                    last = dve.bn_aggr(mv[:, n, t, :], bn[:, n, t, :])
                last.then_inc(mv_done[n], 1)
                dve.wait_ge(mv_done[n], g + 1)
                dve.tensor_scalar(ve[:, n, tiles(g)], mv[:, n, tiles(g), 1], LN_EPS, None, ALU.add
                                  ).then_inc(var_ready[n], 1)

            def normalise(n, g):
                dve.wait_ge(rstd_ready[n], g + 1)
                for t in range(g * GT, (g + 1) * GT):
                    last = dve.tensor_scalar(xn[:, t, :], x_sb[:, t, :], mv[:, n, t, 0:1], rstd[:, n, t:t + 1],
                                             ALU.subtract, ALU.mult)
                last.then_inc(xn_ready[n], 1)

            def decay_params():
                dve.wait_ge(exps_done, 2)
                dve.tensor_tensor(a_dt[:, :], exp_a[:, :], dt_sb[:, :], ALU.mult).then_inc(adt_done, 1)
                dve.tensor_tensor(dt_bias[:, :], cols_sb[:, 2:3], dt_sb[:, :], ALU.mult).then_inc(adt_done, 1)
                dve.wait_ge(sigc_done, 1)
                dve.tensor_tensor(silu_c[:, :], cols_sb[:, 0:1], sig_c[:, :], ALU.mult).then_inc(siluc_done, 1)
                dve.wait_ge(siluc_done, 1)
                dve.wait_ge(consts_set, 6)
                dve.tensor_scalar(silu_rep[:, :], ones[:, :], silu_c[:, 0:1], None, ALU.mult
                                  ).then_inc(siluc_done, 1)

            def modulation():
                dve.wait_ge(mod_product, 1)
                m = ps[:, B_MOD, 0:M_ALL]
                dve.tensor_copy(mod[:, :], m)
                dve.tensor_scalar(mod_p1[:, :], m, 1.0, None, ALU.add).then_inc(mod_ready, 1)
                dve.wait_ge(mod_ready, 1)
                dve.scalar_tensor_tensor(out=mod_abs[:, :], in0=m, scalar=-1.0, in1=mod[:, :],
                                         op0=ALU.mult, op1=ALU.max).then_inc(mod_read, 1)
                dve.tensor_scalar(mod_sgn[:, :], m, 0.0, 2.0, ALU.is_ge, ALU.mult).then_inc(mod_read, 1)
                dve.wait_ge(mod_read, 1)
                dve.tensor_scalar(mod_mag[:, :], mod_abs[:, :], GATE_FLOOR, None, ALU.max).then_inc(mod_read, 1)
                dve.wait_ge(mod_read, 3)
                dve.scalar_tensor_tensor(out=mod_gate[:, :], in0=mod_sgn[:, :], scalar=-1.0,
                                         in1=mod_mag[:, :], op0=ALU.add, op1=ALU.mult).then_inc(mod_read, 1)
                dve.wait_ge(rows_loaded, 16)
                dve.tensor_tensor(bias_sum[:, :], rows_sb[:, O_BC:O_BC + H], rows_sb[:, O_BD:O_BD + H],
                                  ALU.add).then_inc(bias_part, 1)
                dve.wait_ge(proj_loaded, 16)
                dve.wait_ge(mod_read, 4)
                ga = mod_gate[:, 0:H]
                dve.tensor_tensor(wc_g[:, :], proj_sb[:, O_WC:O_WC + H], ga, ALU.mult).then_inc(mixer_weights, 1)
                dve.tensor_tensor(wd_g[:, :], proj_sb[:, O_WD:O_WD + H], ga, ALU.mult).then_inc(mixer_weights, 1)
                dve.wait_ge(bias_part, 1)
                dve.tensor_tensor(bias_g[:, :], bias_sum[:, :], ga, ALU.mult).then_inc(mixer_weights, 1)

            def scan(g):
                if g == 0:
                    dve.wait_ge(abar_done, 1)
                else:
                    dve.wait_ge(states_ready, g)
                dve.wait_ge(bu_ready, g + 1)
                initial = 0.0 if g == 0 else stT[:, g * BANK - 1:g * BANK]
                dve.tensor_tensor_scan(stT[:, tok(g)], a_bar[:, 0:1].to_broadcast((P, BANK)), buT[:, tok(g)],
                                       initial, ALU.mult, ALU.add).then_inc(states_ready, 1)

            def add_mixer(g):
                dve.wait_ge(y_done, g + 1)
                dve.wait_ge(xbias_ready, g + 1)
                dve.tensor_tensor(x_sb[:, tiles(g), :], ps[:, B_Y, :].rearrange("p (q h) -> p q h", q=GT),
                                  x_sb[:, tiles(g), :], ALU.add).then_inc(x1_ready, 1)

            def top_eight(g):
                dve.wait_ge(probs_ready, g + 1)
                for t in range(g * GT, (g + 1) * GT):
                    last = dve.max(top8[:, t, :], probs[:, t, :])
                last.then_inc(top8_done, 1)
                dve.wait_ge(top8_done, g + 1)
                for t in range(g * GT, (g + 1) * GT):
                    last = dve.match_replace(rest[:, t, :], top8[:, t, :], probs[:, t, :], 0.0)
                last.then_inc(rest_ready, 1)
                dve.reduce_sum(top_sum[:, tiles(g)], top8[:, tiles(g), :], AX_X).then_inc(sum_done, 1)
                dve.wait_ge(sum_done, 2 * g + 1)
                dve.tensor_scalar(top_sum_e[:, tiles(g)], top_sum[:, tiles(g)], SUM_EPS, None, ALU.add
                                  ).then_inc(sum_done, 1)
                dve.wait_ge(sum_done, 2 * g + 2)
                dve.reciprocal(top_inv[:, tiles(g)], top_sum_e[:, tiles(g)]).then_inc(inv_ready, 1)

            def combine_weights(g):
                dve.wait_ge(inv_ready, g + 1)
                dve.wait_ge(sel_ready, g + 1)
                if g == 0:
                    dve.wait_ge(consts_set, 6)
                for t in range(g * GT, (g + 1) * GT):
                    last = dve.tensor_scalar(comb[:, t, 0:NE], sel[:, t, :], top_inv[:, t:t + 1], SCALE,
                                             ALU.mult, ALU.mult)
                last.then_inc(comb_ready, 1)

            ln_stats(0, 0)
            decay_params()
            normalise(0, 0)
            ln_stats(0, 1)
            modulation()
            normalise(0, 1)
            ln_stats(0, 2)
            scan(0)
            normalise(0, 2)
            ln_stats(0, 3)
            scan(1)
            normalise(0, 3)
            add_mixer(0)
            ln_stats(1, 0)
            scan(2)
            add_mixer(1)
            normalise(1, 0)
            ln_stats(1, 1)
            scan(3)
            add_mixer(2)
            normalise(1, 1)
            ln_stats(1, 2)
            add_mixer(3)
            normalise(1, 2)
            ln_stats(1, 3)
            top_eight(0)
            normalise(1, 3)
            top_eight(1)
            combine_weights(0)
            combine_weights(1)
            top_eight(2)
            top_eight(3)
            combine_weights(2)
            combine_weights(3)

            def gate(j, s, use):
                dve.wait_ge(silu_done, j + 1)
                dve.wait_ge(cb_loaded[s], 32 * use)
                dve.tensor_tensor(slot(s), slot(s), cb[:, s, :].rearrange("p (b n) -> p b n", b=2),
                                  ALU.mult).then_inc(gated, 1)

            def gated_lo(j, s):
                dve.wait_ge(hi_ready, j + 1)
                dve.tensor_tensor(g_lo[:, s, :].rearrange("p (b n) -> p b n", b=2), slot(s),
                                  g_hi[:, s, :].bitcast(F32).rearrange("p (b n) -> p b n", b=2),
                                  ALU.subtract).then_inc(lo_ready, 1)

            def turn(c, i, last):
                for k in range(BODY):
                    j = PAIRS * c + BODY * i + k
                    if not (last and c == CHUNKS - 1 and k == BODY - 1):
                        gate(j + 1, (k + 1) % RING, PAIRS // RING * c + BODY // RING * i + (k + 1) // RING + 1)
                    gated_lo(j, k % RING)

            gate(0, 0, 1)
            for c in range(CHUNKS):
                with dve.Fori(0, TURNS - 1) as i:
                    turn(c, i, False)
                turn(c, TURNS - 1, True)

            for c in range(CHUNKS):
                dve.wait_ge(ffn_turned, c + 1)
                for b in range(GC):
                    g = GC * c + b
                    dve.tensor_tensor(out_sb[:, tiles(g), :],
                                      ps[:, 2 * c + b, :].rearrange("p (q h) -> p q h", q=GT),
                                      x_sb[:, tiles(g), :], ALU.add).then_inc(out_ready, 1)

        @block.tensor
        def _(pe):
            def modulation():
                pe.wait_ge(wmod_loaded, 16)
                pe.wait_ge(siluc_done, 2)
                pe.matmul(ps[:, B_MOD, 0:H], silu_rep[:, :], wmod_sb[:, GA * H:(GA + 1) * H], start=True, stop=True)
                for m in range(6):
                    last = pe.matmul(ps[:, B_MOD, M_COL + m:M_COL + m + 1], wmod_sb[:, m * H:(m + 1) * H],
                                     silu_c[:, :], start=True, stop=True)
                last.then_inc(mod_product, 1)

            def turn_tokens(n, g):
                if n == 0 and g == 0:
                    pe.wait_ge(ident_set, 1)
                pe.wait_ge(xn_ready[n], g + 1)
                if g > 0:
                    pe.wait_ge(h2_hi_ready if n else hT_ready, g)
                for q in range(GT):
                    last = pe.transpose(ps[:, B_H2T if n else B_XT, q * P:(q + 1) * P], xn[:, g * GT + q, :],
                                        ident[:, :])
                last.then_inc(xT_done[n], 1)

            def project_b(g):
                if g == 0:
                    pe.wait_ge(proj_loaded, 16)
                pe.wait_ge(hT_ready, g + 1)
                if g > 0:
                    pe.wait_ge(bu_ready, g)
                pe.matmul(ps[:, B_BU, :], proj_sb[:, O_WB:O_WB + P], hT[:, tok(g)], start=True, stop=True
                          ).then_inc(bu_done, 1)

            def project_y(g):
                if g == 0:
                    pe.wait_ge(mixer_weights, 2)
                else:
                    pe.wait_ge(x1_ready, g)
                pe.wait_ge(states_ready, g + 1)
                for q in range(GT):
                    cols = slice(g * BANK + q * P, g * BANK + (q + 1) * P)
                    dst = ps[:, B_Y, q * P:(q + 1) * P]
                    pe.matmul(dst, hT[:, cols], wd_g[:, :], start=True, stop=False)
                    last = pe.matmul(dst, stT[:, cols], wc_g[:, :], start=False, stop=True)
                last.then_inc(y_done, 1)

            def route(g):
                if g == 0:
                    pe.wait_ge(rows_loaded, 16)
                    pe.wait_ge(consts_set, 6)
                else:
                    pe.wait_ge(probs_ready, g)
                pe.wait_ge(h2T_ready, g + 1)
                for q in range(GT):
                    cols = slice(g * BANK + q * P, g * BANK + (q + 1) * P)
                    dst = ps[:, B_LOGIT + q // 2, (q % 2) * NE:(q % 2 + 1) * NE]
                    pe.matmul(dst, h2T[:, cols], proj_sb[:, O_RT:O_RT + NE], start=True, stop=False)
                    last = pe.matmul(dst, ones[0:1, 0:P], rows_sb[0:1, O_EB:O_EB + NE], start=False, stop=True)
                last.then_inc(logits_done, 1)

            def turn_combine(g):
                pe.wait_ge(comb_ready, g + 1)
                if g > 0:
                    pe.wait_ge(combT_ready, g)
                for q in range(GT):
                    t = g * GT + q
                    pe.transpose(ps[:, B_CTA, q * P:(q + 1) * P], comb[:, t, 0:P], ident[:, :])
                    last = pe.transpose(ps[0:EC - P, B_CTB, q * P:(q + 1) * P], comb[:, t, P:EC], ident[:, :])
                last.then_inc(combT_done, 1)

            modulation()
            turn_tokens(0, 0)
            turn_tokens(0, 1)
            project_b(0)
            turn_tokens(0, 2)
            project_b(1)
            project_y(0)
            turn_tokens(0, 3)
            project_b(2)
            project_y(1)
            project_b(3)
            turn_tokens(1, 0)
            project_y(2)
            route(0)
            turn_tokens(1, 1)
            project_y(3)
            route(1)
            turn_tokens(1, 2)
            route(2)
            turn_combine(0)
            turn_tokens(1, 3)
            turn_combine(1)
            route(3)
            turn_combine(2)
            turn_combine(3)

            def inner(c, k):
                s = k % RING
                cols = slice(k % WG * P, (k % WG + 1) * P)
                hi, lo = w_hi[:, k // WG % RING, cols], w_lo[:, k // WG % RING, cols]
                for n, (w, v) in enumerate(((hi, h2_hi), (hi, h2_lo), (lo, h2_hi))):
                    for b in range(2):
                        last = pe.matmul(ps[:, 2 * s + b, :], w, v[:, c * CHUNK + b * BANK:c * CHUNK + (b + 1) * BANK],
                                         start=(n == 0), stop=(n == 2))
                last.then_inc(z_ready, 1)

            def down(j, k, end):
                s = k % RING
                base = WG * P + (k % WG) * P
                hi = w_hi[:, k // WG % RING, base:base + P]
                lo = w_lo[:, k // WG % RING, base:base + P]
                pe.wait_ge(hi_ready, j + 1)
                for n, (w, v) in enumerate(((hi, g_hi), (lo, g_hi), (hi, g_lo))):
                    if n == 2:
                        pe.wait_ge(lo_ready, j + 1)
                    for b in range(2):
                        last = pe.matmul(ps[:, B_ACC + b, :], w, v[:, s, b * BANK:(b + 1) * BANK],
                                         start=False, stop=(end and n == 2))
                last.then_inc(down_done, 1)

            def clear_acc(c):
                if c > 0:
                    pe.wait_ge(acc_read, c)
                for b in range(2):
                    pe.matmul(ps[:, B_ACC + b, :], zeros_r[:, :], h2_hi[:, b * BANK:(b + 1) * BANK],
                              start=True, stop=False)

            def next_inner(c, i, k, last):
                ahead = k + RING
                chunk = c
                if last and ahead >= BODY:
                    if c == CHUNKS - 1:
                        return
                    chunk = c + 1
                if ahead % WG == 0:
                    pe.wait_ge(w_split, WGROUPS * c + WG * i + ahead // WG + 1)
                inner(chunk, ahead)

            def turn(c, i, last):
                for k in range(BODY):
                    down(PAIRS * c + BODY * i + k, k, last and k == BODY - 1)
                    next_inner(c, i, k, last)

            pe.wait_ge(combT_ready, GROUPS)
            pe.wait_ge(h2_hi_ready, GROUPS)
            pe.wait_ge(h2_lo_ready, GROUPS)
            pe.wait_ge(w_split, 1)
            for k in range(RING):
                inner(0, k)
            for c in range(CHUNKS):
                clear_acc(c)
                with pe.Fori(0, TURNS - 1) as i:
                    turn(c, i, False)
                turn(c, TURNS - 1, True)
                if c == CHUNKS - 1:
                    for d in range(CHUNKS):
                        pe.wait_ge(acc_read, d + 1)
                        for t in range(CHUNK // P):
                            last = pe.transpose(ps[:, 2 * d + t // GT, t % GT * P:(t % GT + 1) * P],
                                                ffT[:, d * CHUNK + t * P:d * CHUNK + (t + 1) * P], ident[:, :])
                        last.then_inc(ffn_turned, 1)


def kernel(L0_attn_u, L0_attn_log_A, L0_attn_W_B, L0_attn_b_B, L0_attn_W_C, L0_attn_b_C, L0_attn_W_D, L0_attn_b_D,
           L0_attn_log_dt, L0_ffn_router_w, L0_ffn_expert_bias, L0_ffn_w_gate, L0_ffn_w_down,
           L0_ffn_w_gate_shared, L0_ffn_w_down_shared, L0_c, L0_wmod):
    import numpy as np
    import concourse.bacc as bacc
    from concourse.bass_utils import run_bass_kernel_spmd

    def arr(a):
        return np.asarray(a)

    gate = np.concatenate([arr(L0_ffn_w_gate), arr(L0_ffn_w_gate_shared)[None],
                           np.zeros((1, INTER, H), np.float32)])
    down = np.concatenate([arr(L0_ffn_w_down), arr(L0_ffn_w_down_shared)[None],
                           np.zeros((1, H, INTER), np.float32)])
    gate = gate.reshape(WGROUPS, WG, P, H).transpose(0, 3, 1, 2).reshape(WGROUPS, P, WG * P)
    down = down.transpose(0, 2, 1).reshape(WGROUPS, WG, P, H).transpose(0, 2, 1, 3).reshape(WGROUPS, P, WG * P)
    arrays = {
        "x": arr(L0_attn_u),
        "columns": np.stack([arr(L0_c)[0], arr(L0_attn_log_A), arr(L0_attn_b_B)], axis=1),
        "log_dt": arr(L0_attn_log_dt).reshape(1, 1),
        "rows": np.concatenate([arr(L0_attn_b_C), arr(L0_attn_b_D), arr(L0_ffn_expert_bias)])[None],
        "wmod": arr(L0_wmod),
        "proj": np.concatenate([arr(L0_attn_W_B).T, arr(L0_attn_W_C).T, arr(L0_attn_W_D).T,
                                arr(L0_ffn_router_w).T], axis=1),
        "experts": np.concatenate([gate, down], axis=2),
    }
    arrays = {n: np.ascontiguousarray(a) for n, a in arrays.items()}
    nc = bacc.Bacc("TRN2", target_bir_lowering=False, num_devices=1)
    args = [nc.dram_tensor(n, a.shape, F32, kind="ExternalInput").ap() for n, a in arrays.items()]
    out = nc.dram_tensor("out", (1, T, H), F32, kind="ExternalOutput").ap()
    adaln_layer(nc, *args, out)
    r = run_bass_kernel_spmd(nc, [arrays], core_ids=[0])
    return r.results[0]["out"]
```

```python
from contextlib import ExitStack

import concourse.bass as bass
from concourse import mybir

F32 = mybir.dt.float32
F32R = mybir.dt.float32r
ALU = mybir.AluOpType
ACT = mybir.ActivationFunctionType
AX_X = mybir.AxisListType.X

P = 128
T = 2048
H = 128
NE = 160
INTER = 64
TOPK = 8
SCALE = 2.5
LN_EPS = 1e-5
SUM_EPS = 1e-9
GATE_FLOOR = 0.25

BANK = 512
TILES = T // P
GT = BANK // P
GROUPS = T // BANK
CHUNK = 2 * BANK
CHUNKS = T // CHUNK
GC = GROUPS // CHUNKS

EC = NE + 2
PAIRS = EC // 2
WG = 3
WGROUPS = PAIRS // WG
RING = 3
BODY = RING * WG
TURNS = PAIRS // BODY
LEAD = 3
ALL_PAIRS = CHUNKS * PAIRS
ALL_WGROUPS = CHUNKS * WGROUPS

O_WB, O_WC, O_WD, O_RT = 0, 128, 256, 384
SA, CA, GA, SB, CB, GB = range(6)
AS_COLUMN = (SA, CA, SB, CB, GB)
M_COL = {m: H + n for n, m in enumerate(AS_COLUMN)}
M_ALL = H + len(AS_COLUMN)
O_BC, O_BD, O_EB = 0, 128, 256

assert PAIRS == TURNS * BODY and WGROUPS * WG == PAIRS


def adaln_layer(nc: bass.Bass, x: bass.AP, columns: bass.AP, log_dt: bass.AP, rows: bass.AP,
                wmod: bass.AP, proj: bass.AP, experts: bass.AP, out: bass.AP):
    ctx = ExitStack()
    with ctx:
        def sb(name, shape, dt=F32):
            return ctx.enter_context(nc.sbuf_tensor(name, shape, dt))

        def sem(name):
            return ctx.enter_context(nc.semaphore(name))

        cols_sb = sb("cols_sb", [P, 3])
        logdt_sb = sb("logdt_sb", [P, 1])
        rows_sb = sb("rows_sb", [P, 2 * H + NE])
        wmod_sb = sb("wmod_sb", [P, 6 * H])
        proj_sb = sb("proj_sb", [P, 3 * H + NE])
        ident = sb("ident", [P, P])
        ones = sb("ones", [P, P])
        neg_half = sb("neg_half", [P, GT])
        zeros_r = sb("zeros_r", [P, P], F32R)
        exp_a = sb("exp_a", [P, 1])
        dt_sb = sb("dt_sb", [P, 1])
        a_dt = sb("a_dt", [P, 1])
        a_bar = sb("a_bar", [P, 1])
        dt_bias = sb("dt_bias", [P, 1])
        exp_c = sb("exp_c", [P, 1])
        exp_c1 = sb("exp_c1", [P, 1])
        sig_c = sb("sig_c", [P, 1])
        silu_c = sb("silu_c", [P, 1])
        silu_rep = sb("silu_rep", [P, P])
        mod = sb("mod", [P, M_ALL])
        mod_p1 = sb("mod_p1", [P, M_ALL])
        mod_abs = sb("mod_abs", [P, M_ALL])
        mod_mag = sb("mod_mag", [P, M_ALL])
        mod_sgn = sb("mod_sgn", [P, M_ALL])
        mod_gate = sb("mod_gate", [P, M_ALL])
        wc_g = sb("wc_g", [P, H])
        wd_g = sb("wd_g", [P, H])
        bias_sum = sb("bias_sum", [P, H])
        bias_g = sb("bias_g", [P, H])
        x_sb = sb("x_sb", [P, TILES, H])
        xn = sb("xn", [P, TILES, H])
        bn = sb("bn", [P, 2, TILES, 6])
        mv = sb("mv", [P, 2, TILES, 2])
        ve = sb("ve", [P, 2, TILES])
        rstd = sb("rstd", [P, 2, TILES])
        neg_mean = sb("neg_mean", [P, TILES])
        shift = sb("shift", [P, TILES])
        hT = sb("hT", [P, T])
        buT = sb("buT", [P, T])
        stT = sb("stT", [P, T])
        h2T = sb("h2T", [P, T])
        h2_hi = sb("h2_hi", [P, T], F32R)
        h2_lo = sb("h2_lo", [P, T], F32R)
        probs = sb("probs", [P, TILES, NE])
        picked = sb("picked", [P, TILES, NE])
        top8 = sb("top8", [P, TILES, TOPK])
        top_sum = sb("top_sum", [P, TILES])
        top_sum_s = sb("top_sum_s", [P, TILES])
        top_inv = sb("top_inv", [P, TILES])
        comb = sb("comb", [P, TILES, EC])
        combT_a = sb("combT_a", [P, T])
        combT_b = sb("combT_b", [EC - P, T])
        cb = sb("cb", [P, RING, CHUNK])
        w_raw = sb("w_raw", [P, RING, 2 * WG * P])
        w_hi = sb("w_hi", [P, RING, 2 * WG * P], F32R)
        w_lo = sb("w_lo", [P, RING, 2 * WG * P], F32R)
        gu = sb("gu", [P, RING, CHUNK])
        g_hi = sb("g_hi", [P, RING, CHUNK], F32R)
        g_lo = sb("g_lo", [P, RING, CHUNK], F32R)
        ffT, out_sb = buT, xn

        comb_dram = nc.dram_tensor("combine_scratch", (CHUNKS, EC, CHUNK), F32, kind="Internal").ap()
        comb_rows = comb_dram.rearrange("c e t -> (c e) t")

        ps = ctx.enter_context(nc.psum_tensor("ps", [P, 8, BANK], F32))
        B_ACC = 6

        def slot(z):
            return ps[:, 2 * z:2 * z + 2, :]

        B_XT, B_BU, B_Y, B_H2T, B_LOGIT, B_MOD = 0, 1, 2, 3, 4, 7
        B_COMBT = [6, 6, 4, 4]
        FIRST_SLOTS = [0, 1, 0, 1, 0, 1, 0, 1, 2, 0, 1, 2]

        cols_loaded = sem("cols_loaded")
        rows_loaded = sem("rows_loaded")
        wmod_loaded = sem("wmod_loaded")
        proj_loaded = sem("proj_loaded")
        x_loaded = [sem(f"x_loaded{g}") for g in range(GROUPS)]
        w_loaded = [sem(f"w_loaded{s}") for s in range(RING)]
        cb_loaded = [sem(f"cb_loaded{s}") for s in range(RING)]
        comb_stored = [sem(f"comb_stored{c}") for c in range(CHUNKS)]
        out_stored = sem("out_stored")
        consts_set = sem("consts_set")
        ident_set = sem("ident_set")
        exps_done = sem("exps_done")
        adt_done = sem("adt_done")
        abar_done = sem("abar_done")
        siluc_done = sem("siluc_done")
        mod_product = sem("mod_product")
        mod_read = sem("mod_read")
        mod_ready = sem("mod_ready")
        bias_part = sem("bias_part")
        mixer_weights = sem("mixer_weights")
        bn_done = [sem(f"bn_done{n}") for n in range(2)]
        mv_done = [sem(f"mv_done{n}") for n in range(2)]
        var_ready = [sem(f"var_ready{n}") for n in range(2)]
        rstd_ready = [sem(f"rstd_ready{n}") for n in range(2)]
        shift_ready = sem("shift_ready")
        xn_ready = [sem(f"xn_ready{n}") for n in range(2)]
        xT_done = [sem(f"xT_done{n}") for n in range(2)]
        hT_ready = sem("hT_ready")
        bu_done = sem("bu_done")
        bu_ready = sem("bu_ready")
        states_ready = sem("states_ready")
        y_done = sem("y_done")
        xbias_ready = sem("xbias_ready")
        x1_ready = sem("x1_ready")
        h2T_ready = sem("h2T_ready")
        h2_hi_ready = sem("h2_hi_ready")
        h2_lo_ready = sem("h2_lo_ready")
        logits_done = sem("logits_done")
        probs_ready = sem("probs_ready")
        top8_done = sem("top8_done")
        rest_ready = sem("rest_ready")
        sum_done = sem("sum_done")
        inv_ready = sem("inv_ready")
        sel_ready = sem("sel_ready")
        comb_ready = sem("comb_ready")
        combT_done = sem("combT_done")
        combT_ready = sem("combT_ready")
        w_hi_done = sem("w_hi_done")
        w_split = sem("w_split")
        z_ready = sem("z_ready")
        silu_done = sem("silu_done")
        gated = sem("gated")
        hi_ready = sem("hi_ready")
        lo_ready = sem("lo_ready")
        down_done = sem("down_done")
        acc_read = sem("acc_read")
        ffn_turned = sem("ffn_turned")
        out_ready = sem("out_ready")

        block = ctx.enter_context(nc.Block())

        def tok(g):
            return slice(g * BANK, (g + 1) * BANK)

        def tiles(g):
            return slice(g * GT, (g + 1) * GT)

        def x_dram(a, g):
            return a[0, tok(g), :].rearrange("(q p) h -> p q h", p=P)

        @block.sync
        def _(sp):
            for g in range(GROUPS):
                sp.dma_start(x_sb[:, tiles(g), :], x_dram(x, g)).then_inc(x_loaded[g], 16)
                if g == 0:
                    sp.dma_start(proj_sb[:, :], proj).then_inc(proj_loaded, 16)

            def load_weights(group, s):
                sp.dma_start(w_raw[:, s, :], experts[bass.ds(group, 1), :, :].rearrange("a p n -> (a p) n")
                             ).then_inc(w_loaded[s], 16)

            def load_combine(pair, s):
                for half in range(2):
                    row = comb_rows[bass.ds(2 * pair + half, 1), :]
                    sp.dma_start(cb[INTER * half:INTER * (half + 1), s, :],
                                 row.to_broadcast((INTER, CHUNK))).then_inc(cb_loaded[s], 16)

            for group in range(RING):
                load_weights(group, group)
            sp.wait_ge(combT_ready, GC)
            sp.dma_start(comb_dram[0, 0:P, :], combT_a[:, 0:CHUNK]).then_inc(comb_stored[0], 16)
            sp.dma_start(comb_dram[0, P:EC, :], combT_b[:, 0:CHUNK]).then_inc(comb_stored[0], 16)
            sp.wait_ge(comb_stored[0], 32)
            for pair in range(RING):
                load_combine(pair, pair)

            def turn(c, i, last):
                for k in range(BODY):
                    j = PAIRS * c + BODY * i + k
                    if k % WG == 0 and not (last and c == CHUNKS - 1):
                        group = WGROUPS * c + WG * i + k // WG
                        sp.wait_ge(w_split, group + 1)
                        nxt = k // WG if last else WG * i + k // WG + RING
                        load_weights(nxt, k // WG)
                    if not (last and c == CHUNKS - 1 and k + RING >= BODY):
                        sp.wait_ge(gated, j + 1)
                        load_combine(j + RING, k % RING)

            for c in range(CHUNKS):
                with sp.Fori(0, TURNS - 1) as i:
                    turn(c, i, False)
                if c == 0:
                    sp.wait_ge(comb_stored[1], 32)
                turn(c, TURNS - 1, True)

            for g in range(GROUPS):
                sp.wait_ge(out_ready, g + 1)
                sp.dma_start(x_dram(out, g), out_sb[:, tiles(g), :]).then_inc(out_stored, 16)
            sp.wait_ge(out_stored, 16 * GROUPS)

        @block.gpsimd
        def _(pool):
            pool.memset(ident[:, :], 0.0).then_inc(consts_set, 1)
            pool.memset(neg_half[:, :], -0.5).then_inc(consts_set, 1)
            pool.memset(ones[:, :], 1.0).then_inc(consts_set, 1)
            pool.memset(zeros_r[:, :].bitcast(F32), 0.0).then_inc(consts_set, 1)
            pool.memset(comb[:, :, NE:NE + 1], 1.0).then_inc(consts_set, 1)
            pool.memset(comb[:, :, NE + 1:EC], 0.0).then_inc(consts_set, 1)
            pool.wait_ge(consts_set, 6)
            pool.affine_select(out=ident[:, :], in_=ident[:, :], compare_op=ALU.not_equal, fill=1.0,
                               base=0, pattern=[[-1, P]], channel_multiplier=1).then_inc(ident_set, 1)

            def inv_std_1(g):
                pool.wait_ge(var_ready[0], g + 1)
                pool.tensor_tensor(rstd[:, 0, tiles(g)], ve[:, 0, tiles(g)], neg_half[:, :],
                                   ALU.pow).then_inc(rstd_ready[0], 1)

            def inv_std_2(g):
                pool.wait_ge(var_ready[1], g + 1)
                pool.tensor_tensor(rstd[:, 1, tiles(g)], ve[:, 1, tiles(g)], neg_half[:, :],
                                   ALU.pow).then_inc(rstd_ready[1], 1)
                pool.wait_ge(rstd_ready[1], g + 1)
                pool.tensor_tensor(shift[:, tiles(g)], neg_mean[:, tiles(g)], rstd[:, 1, tiles(g)],
                                   ALU.mult).then_inc(shift_ready, 1)

            def add_bias(g):
                if g == 0:
                    pool.wait_ge(mixer_weights, 3)
                pool.wait_ge(xn_ready[0], g + 1)
                pool.tensor_tensor(x_sb[:, tiles(g), :], x_sb[:, tiles(g), :],
                                   bias_g[:, :].rearrange("p (a h) -> p a h", a=1).to_broadcast((P, GT, H)),
                                   ALU.add).then_inc(xbias_ready, 1)

            def input_lo(g):
                pool.wait_ge(h2T_ready, g + 1)
                pool.wait_ge(h2_hi_ready, g + 1)
                pool.tensor_tensor(h2_lo[:, tok(g)], h2T[:, tok(g)], h2_hi[:, tok(g)].bitcast(F32),
                                   ALU.subtract).then_inc(h2_lo_ready, 1)

            def select(g):
                pool.wait_ge(rest_ready, g + 1)
                pool.tensor_tensor(picked[:, tiles(g), :], probs[:, tiles(g), :], picked[:, tiles(g), :],
                                   ALU.subtract).then_inc(sel_ready, 1)

            def split_weights(group, s, use):
                pool.wait_ge(w_loaded[s], 16 * use)
                pool.tensor_tensor(w_hi[:, s, :].rearrange("p (a n) -> p a n", n=P),
                                   w_raw[:, s, :].rearrange("p (a n) -> p a n", n=P),
                                   ones[:, :].rearrange("p (a n) -> p a n", a=1).to_broadcast((P, 2 * WG, P)),
                                   ALU.mult).then_inc(w_hi_done, 1)
                pool.wait_ge(w_hi_done, group + 1)
                pool.tensor_tensor(w_lo[:, s, :], w_raw[:, s, :], w_hi[:, s, :].bitcast(F32),
                                   ALU.subtract).then_inc(w_split, 1)

            def first_split(group):
                split_weights(group, group, 1)

            for stage, n in (
                    (inv_std_1, 0), (inv_std_1, 1), (inv_std_1, 2), (inv_std_1, 3), (first_split, 0),
                    (add_bias, 0), (add_bias, 1), (add_bias, 2), (add_bias, 3), (inv_std_2, 0),
                    (inv_std_2, 1), (inv_std_2, 2), (input_lo, 0), (select, 0), (input_lo, 1),
                    (inv_std_2, 3), (input_lo, 2), (select, 1), (first_split, 1), (select, 2),
                    (input_lo, 3), (select, 3), (first_split, 2)):
                stage(n)

            def turn(c, i, last):
                for s in range(BODY // WG):
                    if last and c == CHUNKS - 1:
                        continue
                    group = WGROUPS * c + WG * i + s
                    pool.wait_ge(down_done, WG * (group + 1))
                    split_weights(group + RING, s, WGROUPS // RING * c + i + 2)

            for c in range(CHUNKS):
                with pool.Fori(0, TURNS - 1) as i:
                    turn(c, i, False)
                turn(c, TURNS - 1, True)

        @block.scalar
        def _(act):
            act.dma_start(cols_sb[:, :], columns).then_inc(cols_loaded, 16)
            act.dma_start(logdt_sb[:, :], log_dt.to_broadcast((P, 1))).then_inc(cols_loaded, 16)
            act.dma_start(wmod_sb[:, :], wmod).then_inc(wmod_loaded, 16)
            act.dma_start(rows_sb[:, :], rows.to_broadcast((P, 2 * H + NE))).then_inc(rows_loaded, 16)
            act.wait_ge(cols_loaded, 32)
            act.activation(exp_c[:, :], cols_sb[:, 0:1], ACT.Exp, scale=-1.0).then_inc(exps_done, 1)
            act.activation(dt_sb[:, :], logdt_sb[:, :], ACT.Exp).then_inc(exps_done, 1)
            act.activation(exp_a[:, :], cols_sb[:, 1:2], ACT.Exp).then_inc(exps_done, 1)
            act.wait_ge(adt_done, 1)
            act.activation(a_bar[:, :], a_dt[:, :], ACT.Exp, scale=-1.0).then_inc(abar_done, 1)

            def modulate_1(g):
                if g == 0:
                    act.wait_ge(mod_ready, 1)
                act.wait_ge(xT_done[0], g + 1)
                act.activation(hT[:, tok(g)], ps[:, B_XT, :], ACT.Identity,
                               bias=mod[:, M_COL[SA]:M_COL[SA] + 1],
                               scale=mod_p1[:, M_COL[CA]:M_COL[CA] + 1]).then_inc(hT_ready, 1)

            def scale_bu(g):
                act.wait_ge(bu_done, g + 1)
                act.activation(buT[:, tok(g)], ps[:, B_BU, :], ACT.Identity, bias=dt_bias[:, :],
                               scale=dt_sb[:, :]).then_inc(bu_ready, 1)

            def normalise_2(g):
                act.wait_ge(shift_ready, g + 1)
                act.wait_ge(x1_ready, g + 1)
                act.wait_ge(xT_done[0], g + 1)
                for t in range(g * GT, (g + 1) * GT):
                    last = act.activation(xn[:, t, :], x_sb[:, t, :], ACT.Identity, bias=shift[:, t:t + 1],
                                          scale=rstd[:, 1, t:t + 1])
                last.then_inc(xn_ready[1], 1)

            def modulate_2(g):
                act.wait_ge(xT_done[1], g + 1)
                for dst, done in ((h2T, h2T_ready), (h2_hi, h2_hi_ready)):
                    act.activation(dst[:, tok(g)], ps[:, B_H2T, :], ACT.Identity,
                                   bias=mod[:, M_COL[SB]:M_COL[SB] + 1],
                                   scale=mod_p1[:, M_COL[CB]:M_COL[CB] + 1]).then_inc(done, 1)

            def router_probs(g):
                act.wait_ge(logits_done, g + 1)
                act.activation(probs[:, tiles(g), :].rearrange("p (b q) e -> p b (q e)", b=2),
                               ps[:, B_LOGIT:B_LOGIT + 2, 0:2 * NE], ACT.Sigmoid).then_inc(probs_ready, 1)

            def combine_weights(g):
                act.wait_ge(sel_ready, g + 1)
                act.wait_ge(inv_ready, g + 1)
                if g == 0:
                    act.wait_ge(consts_set, 6)
                for t in range(g * GT, (g + 1) * GT):
                    last = act.activation(comb[:, t, 0:NE], picked[:, t, :], ACT.Copy, scale=top_inv[:, t:t + 1])
                last.then_inc(comb_ready, 1)

            def keep_combT(g):
                act.wait_ge(combT_done, g + 1)
                act.activation(combT_a[:, tok(g)], ps[:, B_COMBT[g], :], ACT.Copy)
                act.activation(combT_b[:, tok(g)], ps[0:EC - P, B_COMBT[g] + 1, :], ACT.Copy
                               ).then_inc(combT_ready, 1)

            def store_combine(c):
                act.wait_ge(combT_ready, GC * (c + 1))
                cols = slice(c * CHUNK, (c + 1) * CHUNK)
                act.dma_start(comb_dram[c, 0:P, :], combT_a[:, cols]).then_inc(comb_stored[c], 16)
                act.dma_start(comb_dram[c, P:EC, :], combT_b[:, cols]).then_inc(comb_stored[c], 16)

            def silu(j, z):
                act.wait_ge(z_ready, j + 1)
                act.activation(slot(z), slot(z), ACT.Silu).then_inc(silu_done, 1)

            def gated_hi(j, k):
                act.wait_ge(gated, j + 1)
                if not (isinstance(j, int) and j < RING):
                    act.wait_ge(down_done, j - RING + 1)
                act.activation(g_hi[:, k % RING, :], gu[:, k % RING, :], ACT.Copy).then_inc(hi_ready, 1)

            def keep_sum(c):
                act.wait_ge(down_done, PAIRS * (c + 1))
                for b in range(2):
                    act.activation(ffT[:, c * CHUNK + b * BANK:c * CHUNK + (b + 1) * BANK],
                                   ps[:, B_ACC + b, :], ACT.Copy,
                                   scale=mod_gate[:, M_COL[GB]:M_COL[GB] + 1]).then_inc(acc_read, 1)

            def first_silu(j):
                silu(j, FIRST_SLOTS[j])

            def first_hi(j):
                gated_hi(j, j)

            for stage, n in (
                    (modulate_1, 0), (modulate_1, 1), (scale_bu, 0), (modulate_1, 2), (scale_bu, 1),
                    (modulate_1, 3), (scale_bu, 2), (normalise_2, 0), (scale_bu, 3), (modulate_2, 0),
                    (normalise_2, 1), (router_probs, 0), (modulate_2, 1), (normalise_2, 2),
                    (router_probs, 1), (modulate_2, 2), (combine_weights, 0), (normalise_2, 3),
                    (keep_combT, 0), (router_probs, 2), (combine_weights, 1), (modulate_2, 3),
                    (keep_combT, 1), (router_probs, 3), (first_silu, 0), (first_silu, 1),
                    (combine_weights, 2), (first_hi, 0), (first_silu, 2), (keep_combT, 2), (first_hi, 1),
                    (first_silu, 3), (combine_weights, 3), (first_hi, 2), (first_silu, 4), (first_hi, 3),
                    (first_silu, 5), (keep_combT, 3), (store_combine, 1), (first_hi, 4), (first_silu, 6),
                    (first_hi, 5), (first_silu, 7), (first_hi, 6), (first_silu, 8), (first_hi, 7),
                    (first_silu, 9), (first_hi, 8)):
                stage(n)

            def turn(c, i, last):
                for k in range(BODY):
                    j = PAIRS * c + BODY * i + k
                    if not (last and c == CHUNKS - 1 and k == BODY - 1):
                        silu(j + 1, (k + 1) % RING)
                    gated_hi(j, k)
                    if c > 0 and isinstance(i, int) and i == 0 and k == 0:
                        keep_sum(c - 1)

            for c in range(CHUNKS):
                if c > 0:
                    turn(c, 0, False)
                with act.Fori(1, TURNS - 1) as i:
                    turn(c, i, False)
                turn(c, TURNS - 1, True)
            keep_sum(CHUNKS - 1)

        @block.vector
        def _(dve):
            def stats_1(g):
                ln_stats(0, g)

            def stats_2(g):
                ln_stats(1, g)

            def ln_stats(n, g):
                if n == 0:
                    dve.wait_ge(x_loaded[g], 16)
                else:
                    dve.wait_ge(x1_ready, g + 1)
                for t in range(g * GT, (g + 1) * GT):
                    last = dve.bn_stats(bn[:, n, t, :], x_sb[:, t, :])
                last.then_inc(bn_done[n], 1)
                dve.wait_ge(bn_done[n], g + 1)
                for t in range(g * GT, (g + 1) * GT):
                    last = dve.bn_aggr(mv[:, n, t, :], bn[:, n, t, :])
                last.then_inc(mv_done[n], 1)
                dve.wait_ge(mv_done[n], g + 1)
                if n == 1:
                    dve.tensor_scalar(neg_mean[:, tiles(g)], mv[:, n, tiles(g), 0], -1.0, None, ALU.mult)
                dve.tensor_scalar(ve[:, n, tiles(g)], mv[:, n, tiles(g), 1], LN_EPS, None, ALU.add
                                  ).then_inc(var_ready[n], 1)

            def normalise_1(g):
                dve.wait_ge(rstd_ready[0], g + 1)
                for t in range(g * GT, (g + 1) * GT):
                    last = dve.tensor_scalar(xn[:, t, :], x_sb[:, t, :], mv[:, 0, t, 0:1], rstd[:, 0, t:t + 1],
                                             ALU.subtract, ALU.mult)
                last.then_inc(xn_ready[0], 1)

            def activations():
                dve.wait_ge(exps_done, 1)
                dve.tensor_scalar(exp_c1[:, :], exp_c[:, :], 1.0, None, ALU.add).then_inc(siluc_done, 1)
                dve.wait_ge(siluc_done, 1)
                dve.reciprocal(sig_c[:, :], exp_c1[:, :]).then_inc(siluc_done, 1)
                dve.wait_ge(siluc_done, 2)
                dve.tensor_tensor(silu_c[:, :], cols_sb[:, 0:1], sig_c[:, :], ALU.mult).then_inc(siluc_done, 1)
                dve.wait_ge(siluc_done, 3)
                dve.wait_ge(consts_set, 6)
                dve.tensor_scalar(silu_rep[:, :], ones[:, :], silu_c[:, 0:1], None, ALU.mult
                                  ).then_inc(siluc_done, 1)
                dve.wait_ge(exps_done, 3)
                dve.tensor_tensor(a_dt[:, :], exp_a[:, :], dt_sb[:, :], ALU.mult).then_inc(adt_done, 1)
                dve.tensor_tensor(dt_bias[:, :], cols_sb[:, 2:3], dt_sb[:, :], ALU.mult).then_inc(adt_done, 1)

            def modulation():
                dve.wait_ge(mod_product, 1)
                m = ps[:, B_MOD, 0:M_ALL]
                dve.tensor_copy(mod[:, :], m)
                dve.tensor_scalar(mod_p1[:, :], m, 1.0, None, ALU.add).then_inc(mod_ready, 1)

            def mixer_gate():
                m = ps[:, B_MOD, 0:M_ALL]
                dve.wait_ge(mod_ready, 1)
                dve.scalar_tensor_tensor(out=mod_abs[:, :], in0=m, scalar=-1.0, in1=mod[:, :],
                                         op0=ALU.mult, op1=ALU.max).then_inc(mod_read, 1)
                dve.tensor_scalar(mod_sgn[:, :], m, 0.0, 2.0, ALU.is_ge, ALU.mult).then_inc(mod_read, 1)
                dve.wait_ge(mod_read, 1)
                dve.tensor_scalar(mod_mag[:, :], mod_abs[:, :], GATE_FLOOR, None, ALU.max).then_inc(mod_read, 1)
                dve.wait_ge(mod_read, 3)
                dve.scalar_tensor_tensor(out=mod_gate[:, :], in0=mod_sgn[:, :], scalar=-1.0,
                                         in1=mod_mag[:, :], op0=ALU.add, op1=ALU.mult).then_inc(mod_read, 1)
                dve.wait_ge(rows_loaded, 16)
                dve.tensor_tensor(bias_sum[:, :], rows_sb[:, O_BC:O_BC + H], rows_sb[:, O_BD:O_BD + H],
                                  ALU.add).then_inc(bias_part, 1)
                dve.wait_ge(proj_loaded, 16)
                dve.wait_ge(mod_read, 4)
                ga = mod_gate[:, 0:H]
                dve.tensor_tensor(wc_g[:, :], proj_sb[:, O_WC:O_WC + H], ga, ALU.mult).then_inc(mixer_weights, 1)
                dve.tensor_tensor(wd_g[:, :], proj_sb[:, O_WD:O_WD + H], ga, ALU.mult).then_inc(mixer_weights, 1)
                dve.wait_ge(bias_part, 1)
                dve.tensor_tensor(bias_g[:, :], bias_sum[:, :], ga, ALU.mult).then_inc(mixer_weights, 1)

            def scan(g):
                if g == 0:
                    dve.wait_ge(abar_done, 1)
                else:
                    dve.wait_ge(states_ready, g)
                dve.wait_ge(bu_ready, g + 1)
                initial = 0.0 if g == 0 else stT[:, g * BANK - 1:g * BANK]
                dve.tensor_tensor_scan(stT[:, tok(g)], a_bar[:, 0:1].to_broadcast((P, BANK)), buT[:, tok(g)],
                                       initial, ALU.mult, ALU.add).then_inc(states_ready, 1)

            def add_mixer(g):
                dve.wait_ge(y_done, g + 1)
                dve.wait_ge(xbias_ready, g + 1)
                dve.tensor_tensor(x_sb[:, tiles(g), :], ps[:, B_Y, :].rearrange("p (q h) -> p q h", q=GT),
                                  x_sb[:, tiles(g), :], ALU.add).then_inc(x1_ready, 1)

            def top_eight(g):
                dve.wait_ge(probs_ready, g + 1)
                for t in range(g * GT, (g + 1) * GT):
                    last = dve.max(top8[:, t, :], probs[:, t, :])
                last.then_inc(top8_done, 1)
                dve.wait_ge(top8_done, g + 1)
                for t in range(g * GT, (g + 1) * GT):
                    last = dve.match_replace(picked[:, t, :], top8[:, t, :], probs[:, t, :], 0.0)
                last.then_inc(rest_ready, 1)
                dve.reduce_sum(top_sum[:, tiles(g)], top8[:, tiles(g), :], AX_X).then_inc(sum_done, 1)
                dve.wait_ge(sum_done, 2 * g + 1)
                dve.tensor_scalar(top_sum_s[:, tiles(g)], top_sum[:, tiles(g)], SUM_EPS, 1.0 / SCALE, ALU.add,
                                  ALU.mult).then_inc(sum_done, 1)
                dve.wait_ge(sum_done, 2 * g + 2)
                dve.reciprocal(top_inv[:, tiles(g)], top_sum_s[:, tiles(g)]).then_inc(inv_ready, 1)

            def gate(j, z, k):
                dve.wait_ge(silu_done, j + 1)
                if not (isinstance(j, int) and j < RING):
                    dve.wait_ge(lo_ready, j - RING + 1)
                dve.tensor_tensor(gu[:, k % RING, :].rearrange("p (b n) -> p b n", b=2), slot(z),
                                  cb[:, k % RING, :].rearrange("p (b n) -> p b n", b=2),
                                  ALU.mult).then_inc(gated, 1)

            def gated_lo(j, k):
                dve.wait_ge(hi_ready, j + 1)
                dve.tensor_tensor(g_lo[:, k % RING, :], gu[:, k % RING, :], g_hi[:, k % RING, :].bitcast(F32),
                                  ALU.subtract).then_inc(lo_ready, 1)

            def first_gate(j):
                dve.wait_ge(cb_loaded[j % RING], 32 * (j // RING + 1))
                gate(j, FIRST_SLOTS[j], j)

            def first_lo(j):
                gated_lo(j, j)

            for stage, n in (
                    (stats_1, 0), (stats_1, 1), (activations, None), (normalise_1, 0), (stats_1, 2),
                    (normalise_1, 1), (modulation, None), (stats_1, 3), (normalise_1, 2),
                    (mixer_gate, None), (normalise_1, 3), (scan, 0), (scan, 1), (add_mixer, 0),
                    (stats_2, 0), (scan, 2), (add_mixer, 1), (stats_2, 1), (scan, 3), (add_mixer, 2),
                    (stats_2, 2), (top_eight, 0), (add_mixer, 3), (stats_2, 3), (top_eight, 1),
                    (top_eight, 2), (top_eight, 3), (first_gate, 0), (first_gate, 1), (first_lo, 0),
                    (first_gate, 2), (first_lo, 1), (first_gate, 3), (first_lo, 2), (first_gate, 4),
                    (first_lo, 3), (first_gate, 5), (first_lo, 4), (first_gate, 6), (first_lo, 5),
                    (first_gate, 7), (first_lo, 6), (first_gate, 8), (first_lo, 7), (first_gate, 9),
                    (first_lo, 8)):
                stage(n) if n is not None else stage()

            def turn(c, i, last):
                for k in range(BODY):
                    j = PAIRS * c + BODY * i + k
                    if not (last and c == CHUNKS - 1 and k == BODY - 1):
                        ahead = k + 1
                        use = PAIRS // RING * c + BODY // RING * i + ahead // RING + 1
                        dve.wait_ge(cb_loaded[ahead % RING], 32 * use)
                        gate(j + 1, ahead % RING, ahead)
                    gated_lo(j, k)

            for c in range(CHUNKS):
                if c > 0:
                    turn(c, 0, False)
                with dve.Fori(1, TURNS - 1) as i:
                    turn(c, i, False)
                turn(c, TURNS - 1, True)

            for c in range(CHUNKS):
                for b in range(GC):
                    g = GC * c + b
                    dve.wait_ge(ffn_turned, g + 1)
                    dve.tensor_tensor(out_sb[:, tiles(g), :],
                                      ps[:, 2 * c + b, :].rearrange("p (q h) -> p q h", q=GT),
                                      x_sb[:, tiles(g), :], ALU.add).then_inc(out_ready, 1)

        @block.tensor
        def _(pe):
            def modulation():
                pe.wait_ge(wmod_loaded, 16)
                pe.wait_ge(siluc_done, 4)
                pe.matmul(ps[:, B_MOD, 0:H], silu_rep[:, :], wmod_sb[:, GA * H:(GA + 1) * H], start=True, stop=True)
                for m in AS_COLUMN:
                    last = pe.matmul(ps[:, B_MOD, M_COL[m]:M_COL[m] + 1], wmod_sb[:, m * H:(m + 1) * H],
                                     silu_c[:, :], start=True, stop=True)
                last.then_inc(mod_product, 1)

            def turn_1(g):
                turn_tokens(0, g)

            def turn_2(g):
                turn_tokens(1, g)

            def turn_tokens(n, g):
                if n == 0 and g == 0:
                    pe.wait_ge(ident_set, 1)
                pe.wait_ge(xn_ready[n], g + 1)
                if g > 0:
                    pe.wait_ge(h2_hi_ready if n else hT_ready, g)
                for q in range(GT):
                    last = pe.transpose(ps[:, B_H2T if n else B_XT, q * P:(q + 1) * P], xn[:, g * GT + q, :],
                                        ident[:, :])
                last.then_inc(xT_done[n], 1)

            def project_b(g):
                if g == 0:
                    pe.wait_ge(proj_loaded, 16)
                pe.wait_ge(hT_ready, g + 1)
                if g > 0:
                    pe.wait_ge(bu_ready, g)
                pe.matmul(ps[:, B_BU, :], proj_sb[:, O_WB:O_WB + P], hT[:, tok(g)], start=True, stop=True
                          ).then_inc(bu_done, 1)

            def project_y(g):
                if g == 0:
                    pe.wait_ge(mixer_weights, 2)
                else:
                    pe.wait_ge(x1_ready, g)
                pe.wait_ge(states_ready, g + 1)
                for q in range(GT):
                    cols = slice(g * BANK + q * P, g * BANK + (q + 1) * P)
                    dst = ps[:, B_Y, q * P:(q + 1) * P]
                    pe.matmul(dst, hT[:, cols], wd_g[:, :], start=True, stop=False)
                    last = pe.matmul(dst, stT[:, cols], wc_g[:, :], start=False, stop=True)
                last.then_inc(y_done, 1)

            def route(g):
                if g == 0:
                    pe.wait_ge(rows_loaded, 16)
                    pe.wait_ge(consts_set, 6)
                else:
                    pe.wait_ge(probs_ready, g)
                pe.wait_ge(h2T_ready, g + 1)
                for q in range(GT):
                    cols = slice(g * BANK + q * P, g * BANK + (q + 1) * P)
                    dst = ps[:, B_LOGIT + q // 2, (q % 2) * NE:(q % 2 + 1) * NE]
                    pe.matmul(dst, h2T[:, cols], proj_sb[:, O_RT:O_RT + NE], start=True, stop=False)
                    last = pe.matmul(dst, ones[0:1, 0:P], rows_sb[0:1, O_EB:O_EB + NE], start=False, stop=True)
                last.then_inc(logits_done, 1)

            def turn_combine(g):
                pe.wait_ge(comb_ready, g + 1)
                if g > 0:
                    pe.wait_ge(combT_ready, g)
                if B_COMBT[g] == B_LOGIT:
                    pe.wait_ge(probs_ready, GROUPS)
                if g == 0:
                    pe.wait_ge(mod_read, 3)
                for q in range(GT):
                    t = g * GT + q
                    pe.transpose(ps[:, B_COMBT[g], q * P:(q + 1) * P], comb[:, t, 0:P], ident[:, :])
                    last = pe.transpose(ps[0:EC - P, B_COMBT[g] + 1, q * P:(q + 1) * P], comb[:, t, P:EC],
                                        ident[:, :])
                last.then_inc(combT_done, 1)

            def inner(chunk, z, k):
                cols = slice(k % WG * P, (k % WG + 1) * P)
                hi, lo = w_hi[:, k // WG % RING, cols], w_lo[:, k // WG % RING, cols]
                for n, (w, v) in enumerate(((hi, h2_hi), (hi, h2_lo), (lo, h2_hi))):
                    for b in range(2):
                        last = pe.matmul(ps[:, 2 * z + b, :], w,
                                         v[:, chunk * CHUNK + b * BANK:chunk * CHUNK + (b + 1) * BANK],
                                         start=(n == 0), stop=(n == 2))
                last.then_inc(z_ready, 1)

            def down(j, k, end):
                base = WG * P + k % WG * P
                hi = w_hi[:, k // WG % RING, base:base + P]
                lo = w_lo[:, k // WG % RING, base:base + P]
                pe.wait_ge(hi_ready, j + 1)
                for n, (w, v) in enumerate(((hi, g_hi), (lo, g_hi), (hi, g_lo))):
                    if n == 2:
                        pe.wait_ge(lo_ready, j + 1)
                    for b in range(2):
                        last = pe.matmul(ps[:, B_ACC + b, :], w, v[:, k % RING, b * BANK:(b + 1) * BANK],
                                         start=False, stop=(end and n == 2))
                last.then_inc(down_done, 1)

            def clear_acc(c):
                if c == 0:
                    pe.wait_ge(combT_ready, GC)
                else:
                    pe.wait_ge(acc_read, 2 * c)
                for b in range(2):
                    pe.matmul(ps[:, B_ACC + b, :], zeros_r[:, :], h2_hi[:, b * BANK:(b + 1) * BANK],
                              start=True, stop=False)

            def first_inner(j):
                z = FIRST_SLOTS[j]
                users = [p for p in range(j) if FIRST_SLOTS[p] == z]
                if users:
                    pe.wait_ge(gated, users[-1] + 1)
                elif z == 0:
                    pe.wait_ge(hT_ready, GROUPS)
                    pe.wait_ge(bu_ready, GROUPS)
                elif z == 1:
                    pe.wait_ge(x1_ready, GROUPS)
                    pe.wait_ge(h2_hi_ready, GROUPS)
                else:
                    pe.wait_ge(combT_ready, GROUPS)
                if j == 0:
                    pe.wait_ge(h2_lo_ready, GC)
                if j % WG == 0:
                    pe.wait_ge(w_split, j // WG + 1)
                inner(0, z, j)

            def first_down(j):
                down(j, j, False)

            for stage, n in (
                    (modulation, None), (turn_1, 0), (turn_1, 1), (project_b, 0), (turn_1, 2),
                    (project_b, 1), (project_y, 0), (turn_1, 3), (project_b, 2), (project_y, 1),
                    (project_b, 3), (project_y, 2), (turn_2, 0), (route, 0), (turn_2, 1), (project_y, 3),
                    (route, 1), (turn_2, 2), (route, 2), (turn_combine, 0), (first_inner, 0), (turn_2, 3),
                    (turn_combine, 1), (route, 3), (first_inner, 1), (first_inner, 2), (turn_combine, 2),
                    (first_inner, 3), (clear_acc, 0), (first_down, 0), (first_inner, 4), (first_down, 1),
                    (first_inner, 5), (turn_combine, 3), (first_down, 2), (first_inner, 6),
                    (first_down, 3), (first_inner, 7), (first_down, 4), (first_inner, 8), (first_down, 5),
                    (first_inner, 9), (first_down, 6), (first_inner, 10), (first_down, 7),
                    (first_inner, 11), (first_down, 8)):
                stage(n) if n is not None else stage()

            def next_inner(c, i, k, last):
                ahead = k + LEAD
                chunk = c
                if last and ahead >= BODY:
                    if c == CHUNKS - 1:
                        return
                    chunk = c + 1
                j = PAIRS * c + BODY * i + k
                pe.wait_ge(gated, j + 1)
                if ahead % WG == 0:
                    pe.wait_ge(w_split, WGROUPS * c + WG * i + ahead // WG + 1)
                inner(chunk, ahead % RING, ahead)

            def turn_ffn(c, z):
                for t in range(CHUNK // P):
                    if t % GT == 0:
                        pe.wait_ge(acc_read, 2 * c + t // GT + 1)
                    last = pe.transpose(ps[:, 2 * z + t // GT, t % GT * P:(t % GT + 1) * P],
                                        ffT[:, c * CHUNK + t * P:c * CHUNK + (t + 1) * P], ident[:, :])
                    if t % GT == GT - 1:
                        last.then_inc(ffn_turned, 1)

            def turn(c, i, last):
                for k in range(BODY):
                    next_inner(c, i, k, last)
                    if c > 0 and isinstance(i, int) and i == 0 and k == 0:
                        clear_acc(c)
                    if last and c == CHUNKS - 1 and k == BODY - 1:
                        turn_ffn(0, 0)
                    down(PAIRS * c + BODY * i + k, k, last and k == BODY - 1)

            for c in range(CHUNKS):
                if c > 0:
                    turn(c, 0, False)
                with pe.Fori(1, TURNS - 1) as i:
                    turn(c, i, False)
                if c == 0:
                    pe.wait_ge(h2_lo_ready, GROUPS)
                turn(c, TURNS - 1, True)
            for c in range(1, CHUNKS):
                turn_ffn(c, c)


def kernel(L0_attn_u, L0_attn_log_A, L0_attn_W_B, L0_attn_b_B, L0_attn_W_C, L0_attn_b_C, L0_attn_W_D, L0_attn_b_D,
           L0_attn_log_dt, L0_ffn_router_w, L0_ffn_expert_bias, L0_ffn_w_gate, L0_ffn_w_down,
           L0_ffn_w_gate_shared, L0_ffn_w_down_shared, L0_c, L0_wmod):
    import numpy as np
    import concourse.bacc as bacc
    from concourse.bass_utils import run_bass_kernel_spmd

    def arr(a):
        return np.asarray(a)

    gate = np.concatenate([arr(L0_ffn_w_gate), arr(L0_ffn_w_gate_shared)[None],
                           np.zeros((1, INTER, H), np.float32)])
    down = np.concatenate([arr(L0_ffn_w_down), arr(L0_ffn_w_down_shared)[None],
                           np.zeros((1, H, INTER), np.float32)])
    gate = gate.reshape(WGROUPS, WG, P, H).transpose(0, 3, 1, 2).reshape(WGROUPS, P, WG * P)
    down = down.transpose(0, 2, 1).reshape(WGROUPS, WG, P, H).transpose(0, 2, 1, 3).reshape(WGROUPS, P, WG * P)
    arrays = {
        "x": arr(L0_attn_u),
        "columns": np.stack([arr(L0_c)[0], arr(L0_attn_log_A), arr(L0_attn_b_B)], axis=1),
        "log_dt": arr(L0_attn_log_dt).reshape(1, 1),
        "rows": np.concatenate([arr(L0_attn_b_C), arr(L0_attn_b_D), arr(L0_ffn_expert_bias)])[None],
        "wmod": arr(L0_wmod),
        "proj": np.concatenate([arr(L0_attn_W_B).T, arr(L0_attn_W_C).T, arr(L0_attn_W_D).T,
                                arr(L0_ffn_router_w).T], axis=1),
        "experts": np.concatenate([gate, down], axis=2),
    }
    arrays = {n: np.ascontiguousarray(a) for n, a in arrays.items()}
    nc = bacc.Bacc("TRN2", target_bir_lowering=False, num_devices=1)
    args = [nc.dram_tensor(n, a.shape, F32, kind="ExternalInput").ap() for n, a in arrays.items()]
    out = nc.dram_tensor("out", (1, T, H), F32, kind="ExternalOutput").ap()
    adaln_layer(nc, *args, out)
    r = run_bass_kernel_spmd(nc, [arrays], core_ids=[0])
    return r.results[0]["out"]
```

```python
from contextlib import ExitStack

import concourse.bass as bass
from concourse import mybir

F32 = mybir.dt.float32
F32R = mybir.dt.float32r
ALU = mybir.AluOpType
ACT = mybir.ActivationFunctionType
AX_X = mybir.AxisListType.X

P = 128
T = 2048
H = 128
NE = 160
INTER = 64
TOPK = 8
SCALE = 2.5
LN_EPS = 1e-5
SUM_EPS = 1e-9
HALF = P // 2
GATE_FLOOR = 0.25

BANK = 512
TILES = T // P
GT = BANK // P
GROUPS = T // BANK
CHUNK = 2 * BANK
CHUNKS = T // CHUNK
GC = GROUPS // CHUNKS

SHARED = 2
EC = SHARED + NE
PAIRS = EC // 2
WG = 3
WGROUPS = PAIRS // WG
RING = 3
BODY = RING * WG
TURNS = PAIRS // BODY
LEAD = 3
ALL_PAIRS = CHUNKS * PAIRS
ALL_WGROUPS = CHUNKS * WGROUPS

O_WB, O_WC, O_WD, O_RT = 0, 128, 256, 384
SA, CA, GA, SB, CB, GB = range(6)
AS_COLUMN = (SB, CB, GB)
M_COL = {m: H + n for n, m in enumerate(AS_COLUMN)}
M_ALL = H + len(AS_COLUMN)
O_BC, O_BD, O_EB = 0, 128, 256

WARM_UP = 7
EARLY_ROWS = 32
FIRST_GROUPS = BODY // WG + 2

assert PAIRS == TURNS * BODY and WGROUPS * WG == PAIRS


def adaln_layer(nc: bass.Bass, x: bass.AP, columns: bass.AP, log_dt: bass.AP, rows: bass.AP,
                wmod: bass.AP, proj: bass.AP, experts: bass.AP, out: bass.AP):
    ctx = ExitStack()
    with ctx:
        def sb(name, shape, dt=F32):
            return ctx.enter_context(nc.sbuf_tensor(name, shape, dt))

        def sem(name):
            return ctx.enter_context(nc.semaphore(name))

        cols_sb = sb("cols_sb", [P, 3])
        logdt_sb = sb("logdt_sb", [P, 1])
        rows_sb = sb("rows_sb", [P, 2 * H + NE])
        wmod_sb = sb("wmod_sb", [P, 6 * H])
        proj_sb = sb("proj_sb", [P, 3 * H + NE])
        ident = sb("ident", [P, P])
        ones = sb("ones", [P, P])
        neg_half = sb("neg_half", [P, GT])
        zeros_r = sb("zeros_r", [P, P], F32R)
        share_r = sb("share_r", [P, P], F32R)
        bias_hl = sb("bias_hl", [P, 2, NE], F32R)
        exp_a = sb("exp_a", [P, 1])
        dt_sb = sb("dt_sb", [P, 1])
        a_dt = sb("a_dt", [P, 1])
        a_bar = sb("a_bar", [P, 1])
        dt_bias = sb("dt_bias", [P, 1])
        exp_c = sb("exp_c", [P, 1])
        exp_c1 = sb("exp_c1", [P, 1])
        sig_c = sb("sig_c", [P, 1])
        silu_c = sb("silu_c", [P, 1])
        silu_rep = sb("silu_rep", [P, P])
        sa = sb("sa", [P, 1])
        ca_p1 = sb("ca_p1", [P, 1])
        mod = sb("mod", [P, M_ALL])
        cb_p1 = sb("cb_p1", [P, 1])
        mod_abs = sb("mod_abs", [P, M_ALL])
        mod_mag = sb("mod_mag", [P, M_ALL])
        mod_sgn = sb("mod_sgn", [P, M_ALL])
        mod_gate = sb("mod_gate", [P, M_ALL])
        wc_g = sb("wc_g", [P, H])
        wd_g = sb("wd_g", [P, H])
        bias_sum = sb("bias_sum", [P, H])
        bias_g = sb("bias_g", [P, H])
        x_sb = sb("x_sb", [P, TILES, H])
        xn = sb("xn", [P, TILES, H])
        bn = sb("bn", [P, 2, TILES, 6])
        mv = sb("mv", [P, 2, TILES, 2])
        ve = sb("ve", [P, 2, TILES])
        rstd = sb("rstd", [P, 2, TILES])
        neg_mean = sb("neg_mean", [P, TILES])
        shift = sb("shift", [P, TILES])
        hT = sb("hT", [P, T])
        buT = sb("buT", [P, T])
        stT = sb("stT", [P, T])
        h2T = sb("h2T", [P, T])
        h2_hi = sb("h2_hi", [P, T], F32R)
        h2_lo = sb("h2_lo", [P, T], F32R)
        probs = sb("probs", [P, TILES, NE])
        picked = sb("picked", [P, TILES, NE])
        top8 = sb("top8", [P, TILES, TOPK])
        top_sum = sb("top_sum", [P, TILES])
        top_sum_s = sb("top_sum_s", [P, TILES])
        top_inv = sb("top_inv", [P, TILES])
        comb = sb("comb", [P, TILES, EC])
        combT_a = sb("combT_a", [P, T])
        combT_b = sb("combT_b", [EC - P, T])
        cb = sb("cb", [P, RING, CHUNK])
        w_raw = sb("w_raw", [P, RING, 2 * WG * P])
        w_hi = sb("w_hi", [P, RING, 2 * WG * P], F32R)
        w_lo = sb("w_lo", [P, RING, 2 * WG * P], F32R)
        gu = sb("gu", [P, RING, CHUNK])
        g_hi = sb("g_hi", [P, RING, CHUNK], F32R)
        g_lo = sb("g_lo", [P, RING, CHUNK], F32R)
        ffT, out_sb = buT, xn

        comb_dram = nc.dram_tensor("combine_scratch", (CHUNKS, EC, CHUNK), F32, kind="Internal").ap()
        comb_rows = comb_dram.rearrange("c e t -> (c e) t")

        ps = ctx.enter_context(nc.psum_tensor("ps", [P, 8, BANK], F32))
        B_ACC = 6

        def slot(z):
            return ps[:, 2 * z:2 * z + 2, :]

        B_XT, B_BU, B_Y, B_H2T, B_LOGIT, B_MOD_1, B_MOD = 0, 1, 2, 3, 4, 6, 7
        B_COMBT = [6, 6, 4, 4]
        FIRST_SLOTS = [0, 1, 0, 1, 0, 1, 0, 1, 2, 0, 1, 2]

        cols_loaded = sem("cols_loaded")
        rows_loaded = sem("rows_loaded")
        logdt_loaded = sem("logdt_loaded")
        wmod_loaded = sem("wmod_loaded")
        proj_loaded = sem("proj_loaded")
        x_loaded = [sem(f"x_loaded{g}") for g in range(GROUPS)]
        w_loaded = [sem(f"w_loaded{s}") for s in range(RING)]
        cb_loaded = [sem(f"cb_loaded{s}") for s in range(RING)]
        comb_early_stored = sem("comb_early_stored")
        comb_a_stored = [sem(f"comb_a_stored{c}") for c in range(CHUNKS)]
        comb_b_stored = [sem(f"comb_b_stored{c}") for c in range(CHUNKS)]
        out_stored = sem("out_stored")
        consts_set = sem("consts_set")
        ident_set = sem("ident_set")
        exps_done = sem("exps_done")
        adt_done = sem("adt_done")
        abar_done = sem("abar_done")
        siluc_done = sem("siluc_done")
        mod_product = sem("mod_product")
        mod_1_ready = sem("mod_1_ready")
        mod_read = sem("mod_read")
        mod_ready = sem("mod_ready")
        bias_hi_done = sem("bias_hi_done")
        bias_hl_ready = sem("bias_hl_ready")
        bias_part = sem("bias_part")
        mixer_weights = sem("mixer_weights")
        bn_done = [sem(f"bn_done{n}") for n in range(2)]
        mv_done = [sem(f"mv_done{n}") for n in range(2)]
        var_ready = [sem(f"var_ready{n}") for n in range(2)]
        rstd_ready = [sem(f"rstd_ready{n}") for n in range(2)]
        shift_ready = sem("shift_ready")
        xn_ready = [sem(f"xn_ready{n}") for n in range(2)]
        xT_done = [sem(f"xT_done{n}") for n in range(2)]
        hT_ready = sem("hT_ready")
        bu_done = sem("bu_done")
        bu_ready = sem("bu_ready")
        states_ready = sem("states_ready")
        y_done = sem("y_done")
        xbias_ready = sem("xbias_ready")
        x1_ready = sem("x1_ready")
        h2T_ready = sem("h2T_ready")
        h2_hi_ready = sem("h2_hi_ready")
        h2_lo_ready = sem("h2_lo_ready")
        logits_done = sem("logits_done")
        probs_ready = sem("probs_ready")
        top8_done = sem("top8_done")
        rest_ready = sem("rest_ready")
        sum_done = sem("sum_done")
        inv_ready = sem("inv_ready")
        sel_ready = sem("sel_ready")
        comb_ready = sem("comb_ready")
        combT_done = sem("combT_done")
        combT_a_ready = sem("combT_a_ready")
        combT_b_ready = sem("combT_b_ready")
        w_hi_done = sem("w_hi_done")
        w_hi_ready = sem("w_hi_ready")
        w_split = sem("w_split")
        z_ready = sem("z_ready")
        silu_done = sem("silu_done")
        gated = sem("gated")
        hi_ready = sem("hi_ready")
        lo_ready = sem("lo_ready")
        down_done = sem("down_done")
        half_summed = sem("half_summed")
        acc_read = sem("acc_read")
        last_read = sem("last_read")
        ffn_turned = sem("ffn_turned")
        out_ready = sem("out_ready")

        block = ctx.enter_context(nc.Block())

        def tok(g):
            return slice(g * BANK, (g + 1) * BANK)

        def tiles(g):
            return slice(g * GT, (g + 1) * GT)

        def expert_bias(first, end):
            return (rows_sb[first:end, O_EB:O_EB + NE].rearrange("p (a e) -> p a e", a=1)
                    .to_broadcast((end - first, 2, NE)))

        def x_dram(a, g):
            return a[0, tok(g), :].rearrange("(q p) h -> p q h", p=P)

        @block.sync
        def _(sp):
            for g in range(GROUPS):
                sp.dma_start(x_sb[:, tiles(g), :], x_dram(x, g)).then_inc(x_loaded[g], 16)
                if g == 0:
                    sp.dma_start(wmod_sb[:, :], wmod).then_inc(wmod_loaded, 16)
                elif g == 1:
                    sp.dma_start(logdt_sb[:, :], log_dt.to_broadcast((P, 1))).then_inc(logdt_loaded, 16)
                    sp.dma_start(proj_sb[:, :], proj).then_inc(proj_loaded, 16)
                    sp.dma_start(rows_sb[:, :], rows.to_broadcast((P, 2 * H + NE))).then_inc(rows_loaded, 16)

            def load_weights(group, s):
                sp.dma_start(w_raw[:, s, :], experts[bass.ds(group, 1), :, :].rearrange("a p n -> (a p) n")
                             ).then_inc(w_loaded[s], 16)

            def load_combine(pair, s):
                two = comb_rows[bass.ds(2 * pair, 2), :].rearrange("r (a t) -> r a t", a=1)
                sp.dma_start(cb[:, s, :], two.to_broadcast((2, INTER, CHUNK))).then_inc(cb_loaded[s], 16)

            for group in range(RING):
                load_weights(group, group)
            for g in range(GC):
                sp.wait_ge(combT_a_ready, g + 1)
                sp.dma_start(comb_dram[0, 0:EARLY_ROWS, tok(g)], combT_a[0:EARLY_ROWS, tok(g)]
                             ).then_inc(comb_early_stored, 16)
            sp.dma_start(comb_dram[0, EARLY_ROWS:P, :], combT_a[EARLY_ROWS:P, 0:CHUNK]).then_inc(comb_a_stored[0], 16)
            sp.wait_ge(combT_b_ready, GC)
            sp.dma_start(comb_dram[0, P:EC, :], combT_b[:, 0:CHUNK]).then_inc(comb_b_stored[0], 16)
            sp.wait_ge(comb_early_stored, 16 * GC)
            for pair in range(1, RING):
                load_combine(pair, pair)
            sp.wait_ge(comb_a_stored[0], 16)
            sp.wait_ge(comb_b_stored[0], 16)

            def turn(c, i, last):
                for k in range(BODY):
                    j = PAIRS * c + BODY * i + k
                    if k % WG == 0 and not (last and c == CHUNKS - 1):
                        group = WGROUPS * c + WG * i + k // WG
                        sp.wait_ge(w_split, group + 1)
                        nxt = k // WG if last else WG * i + k // WG + RING
                        load_weights(nxt, k // WG)
                    if not (last and c == CHUNKS - 1 and k + RING >= BODY):
                        sp.wait_ge(gated, j + 1)
                        load_combine(j + RING, k % RING)

            for c in range(CHUNKS):
                with sp.Fori(0, TURNS - 1) as i:
                    turn(c, i, False)
                if c == 0:
                    sp.wait_ge(comb_a_stored[1], 16)
                    sp.wait_ge(comb_b_stored[1], 16)
                turn(c, TURNS - 1, True)

            for g in range(GROUPS - 1):
                sp.wait_ge(out_ready, g + 1)
                sp.dma_start(x_dram(out, g), out_sb[:, tiles(g), :]).then_inc(out_stored, 16)
            for half in range(2):
                q = slice(half * GT // 2, (half + 1) * GT // 2)
                sp.wait_ge(out_ready, GROUPS + half)
                sp.dma_start(x_dram(out, GROUPS - 1)[:, q, :], out_sb[:, tiles(GROUPS - 1), :][:, q, :]
                             ).then_inc(out_stored, 16)
            sp.wait_ge(out_stored, 16 * (GROUPS + 1))

        @block.gpsimd
        def _(pool):
            pool.memset(ident[:, :], 0.0).then_inc(consts_set, 1)
            pool.memset(neg_half[:, :], -0.5).then_inc(consts_set, 1)
            pool.memset(ones[:, :], 1.0).then_inc(consts_set, 1)
            pool.memset(zeros_r[:, :].bitcast(F32), 0.0).then_inc(consts_set, 1)
            pool.memset(share_r[:, :].bitcast(F32), 1.0 / HALF).then_inc(consts_set, 1)
            pool.memset(comb[:, :, 0:1], 1.0).then_inc(consts_set, 1)
            pool.memset(comb[:, :, 1:SHARED], 0.0).then_inc(consts_set, 1)
            pool.wait_ge(consts_set, 7)
            pool.affine_select(out=ident[:, :], in_=ident[:, :], compare_op=ALU.not_equal, fill=1.0,
                               base=0, pattern=[[-1, P]], channel_multiplier=1).then_inc(ident_set, 1)

            def inv_std_1(g):
                pool.wait_ge(var_ready[0], g + 1)
                pool.tensor_tensor(rstd[:, 0, tiles(g)], ve[:, 0, tiles(g)], neg_half[:, :],
                                   ALU.pow).then_inc(rstd_ready[0], 1)

            def inv_std_2(g):
                pool.wait_ge(var_ready[1], g + 1)
                pool.tensor_tensor(rstd[:, 1, tiles(g)], ve[:, 1, tiles(g)], neg_half[:, :],
                                   ALU.pow).then_inc(rstd_ready[1], 1)
                pool.wait_ge(rstd_ready[1], g + 1)
                pool.tensor_tensor(shift[:, tiles(g)], neg_mean[:, tiles(g)], rstd[:, 1, tiles(g)],
                                   ALU.mult).then_inc(shift_ready, 1)

            def add_bias(g):
                if g == 0:
                    pool.wait_ge(mixer_weights, 3)
                pool.wait_ge(xn_ready[0], g + 1)
                pool.tensor_tensor(x_sb[:, tiles(g), :], x_sb[:, tiles(g), :],
                                   bias_g[:, :].rearrange("p (a h) -> p a h", a=1).to_broadcast((P, GT, H)),
                                   ALU.add).then_inc(xbias_ready, 1)

            def input_hi(g):
                pool.wait_ge(h2T_ready, g + 1)
                pool.tensor_tensor(h2_hi[:, tok(g)].rearrange("p (q n) -> p q n", n=P),
                                   h2T[:, tok(g)].rearrange("p (q n) -> p q n", n=P),
                                   ones[:, :].rearrange("p (a n) -> p a n", a=1).to_broadcast((P, GT, P)),
                                   ALU.mult).then_inc(h2_hi_ready, 1)

            def input_lo(g):
                pool.wait_ge(h2_hi_ready, g + 1)
                pool.tensor_tensor(h2_lo[:, tok(g)], h2T[:, tok(g)], h2_hi[:, tok(g)].bitcast(F32),
                                   ALU.subtract).then_inc(h2_lo_ready, 1)

            def first_split(group):
                s = group % RING
                pool.wait_ge(w_loaded[s], 16 * (group // RING + 1))
                if group >= RING:
                    pool.wait_ge(down_done, WG * (group - 2))
                pool.tensor_tensor(w_hi[:, s, :].rearrange("p (a n) -> p a n", n=P),
                                   w_raw[:, s, :].rearrange("p (a n) -> p a n", n=P),
                                   ones[:, :].rearrange("p (a n) -> p a n", a=1).to_broadcast((P, 2 * WG, P)),
                                   ALU.mult).then_inc(w_hi_done, 1)
                pool.wait_ge(w_hi_done, group + 1)
                pool.tensor_tensor(w_lo[:, s, :], w_raw[:, s, :], w_hi[:, s, :].bitcast(F32),
                                   ALU.subtract).then_inc(w_split, 1)

            def weights_lo(group, s):
                pool.wait_ge(w_hi_ready, group - FIRST_GROUPS + 1)
                pair = WG * (group - 2) + 1
                half = WG * P
                for n in range(2):
                    pool.wait_ge(lo_ready, pair + n + 1)
                    cols = slice(n * half, (n + 1) * half)
                    last = pool.tensor_tensor(w_lo[:, s, cols], w_raw[:, s, cols], w_hi[:, s, cols].bitcast(F32),
                                              ALU.subtract)
                last.then_inc(w_split, 1)

            for stage, n in (
                    (inv_std_1, 0), (inv_std_1, 1), (inv_std_1, 2), (first_split, 0), (add_bias, 0),
                    (inv_std_1, 3), (add_bias, 1), (add_bias, 2), (inv_std_2, 0), (add_bias, 3),
                    (inv_std_2, 1), (input_hi, 0), (inv_std_2, 2), (input_hi, 1), (input_lo, 0),
                    (input_lo, 1), (inv_std_2, 3), (input_hi, 2), (input_lo, 2), (first_split, 1),
                    (input_hi, 3), (input_lo, 3), (first_split, 2), (first_split, 3),
                    (first_split, 4)):
                stage(n)

            def turn(c, i, last):
                for s in range(1 if last and c == CHUNKS - 1 else BODY // WG):
                    weights_lo(WGROUPS * c + WG * i + s + 2, (s + 2) % RING)

            for c in range(CHUNKS):
                with pool.Fori(1 if c == 0 else 0, TURNS - 1) as i:
                    turn(c, i, False)
                turn(c, TURNS - 1, True)

        @block.scalar
        def _(act):
            act.dma_start(cols_sb[:, :], columns).then_inc(cols_loaded, 16)
            act.preload_act_table(ACT.Exp)
            act.wait_ge(cols_loaded, 16)
            act.activation(exp_c[:, :], cols_sb[:, 0:1], ACT.Exp, scale=-1.0).then_inc(exps_done, 1)
            act.activation(exp_a[:, :], cols_sb[:, 1:2], ACT.Exp).then_inc(exps_done, 1)
            act.wait_ge(logdt_loaded, 16)
            act.activation(dt_sb[:, :], logdt_sb[:, :], ACT.Exp).then_inc(exps_done, 1)
            act.wait_ge(adt_done, 1)
            act.activation(a_bar[:, :], a_dt[:, :], ACT.Exp, scale=-1.0).then_inc(abar_done, 1)
            act.preload_act_table(ACT.Sigmoid)

            def modulate_1(g):
                if g == 0:
                    act.wait_ge(mod_1_ready, 1)
                act.wait_ge(xT_done[0], g + 1)
                act.activation(hT[:, tok(g)], ps[:, B_XT, :], ACT.Identity, bias=sa[:, :],
                               scale=ca_p1[:, :]).then_inc(hT_ready, 1)

            def bias_hi():
                act.wait_ge(rows_loaded, 16)
                act.activation(bias_hl[:, :, :], expert_bias(0, P), ACT.Copy).then_inc(bias_hi_done, 1)

            def scale_bu(g):
                act.wait_ge(bu_done, g + 1)
                act.activation(buT[:, tok(g)], ps[:, B_BU, :], ACT.Identity, bias=dt_bias[:, :],
                               scale=dt_sb[:, :]).then_inc(bu_ready, 1)

            def normalise_2(g):
                act.wait_ge(shift_ready, g + 1)
                act.wait_ge(x1_ready, g + 1)
                act.wait_ge(xT_done[0], g + 1)
                for t in range(g * GT, (g + 1) * GT):
                    last = act.activation(xn[:, t, :], x_sb[:, t, :], ACT.Identity, bias=shift[:, t:t + 1],
                                          scale=rstd[:, 1, t:t + 1])
                last.then_inc(xn_ready[1], 1)

            def modulate_2(g):
                if g == 0:
                    act.wait_ge(mod_ready, 1)
                act.wait_ge(xT_done[1], g + 1)
                act.activation(h2T[:, tok(g)], ps[:, B_H2T, :], ACT.Identity,
                               bias=mod[:, M_COL[SB]:M_COL[SB] + 1], scale=cb_p1[:, :]).then_inc(h2T_ready, 1)

            def router_probs(g):
                act.wait_ge(logits_done, g + 1)
                act.activation(probs[:, tiles(g), :].rearrange("p (b q) e -> p b (q e)", b=2),
                               ps[:, B_LOGIT:B_LOGIT + 2, 0:2 * NE], ACT.Sigmoid).then_inc(probs_ready, 1)

            def combine_weights(g):
                act.wait_ge(sel_ready, g + 1)
                act.wait_ge(inv_ready, g + 1)
                if g == 0:
                    act.wait_ge(consts_set, 7)
                for t in range(g * GT, (g + 1) * GT):
                    last = act.activation(comb[:, t, SHARED:EC], picked[:, t, :], ACT.Copy, scale=top_inv[:, t:t + 1])
                last.then_inc(comb_ready, 1)

            def keep_combT_a(g):
                act.wait_ge(combT_done, g + 1)
                act.activation(combT_a[:, tok(g)], ps[:, B_COMBT[g], :], ACT.Copy).then_inc(combT_a_ready, 1)

            def keep_combT_b(g):
                act.wait_ge(combT_done, g + 1)
                act.activation(combT_b[:, tok(g)], ps[0:EC - P, B_COMBT[g] + 1, :], ACT.Copy
                               ).then_inc(combT_b_ready, 1)

            def store_combine(c):
                act.wait_ge(combT_a_ready, GC * (c + 1))
                act.wait_ge(combT_b_ready, GC * (c + 1))
                cols = slice(c * CHUNK, (c + 1) * CHUNK)
                act.dma_start(comb_dram[c, 0:P, :], combT_a[:, cols]).then_inc(comb_a_stored[c], 16)
                act.dma_start(comb_dram[c, P:EC, :], combT_b[:, cols]).then_inc(comb_b_stored[c], 16)

            def silu(j, z):
                act.wait_ge(z_ready, j + 1)
                act.activation(slot(z), slot(z), ACT.Silu).then_inc(silu_done, 1)

            def shared_sigmoid():
                act.wait_ge(z_ready, 1)
                act.activation(gu[:, 0, :].rearrange("p (b n) -> p b n", b=2), slot(FIRST_SLOTS[0]), ACT.Sigmoid
                               ).then_inc(silu_done, 1)

            def gated_hi(j, k):
                act.wait_ge(gated, j + 1)
                if not (isinstance(j, int) and j < RING):
                    act.wait_ge(down_done, j - RING + 1)
                act.activation(g_hi[:, k % RING, :], gu[:, k % RING, :], ACT.Copy).then_inc(hi_ready, 1)

            def keep_sum(c):
                if c == CHUNKS - 1:
                    act.wait_ge(half_summed, 1)
                else:
                    act.wait_ge(down_done, PAIRS * (c + 1))
                for b in range(1 if c == CHUNKS - 1 else 2):
                    act.activation(ffT[:, c * CHUNK + b * BANK:c * CHUNK + (b + 1) * BANK],
                                   ps[:, B_ACC + b, :], ACT.Copy,
                                   scale=mod_gate[:, M_COL[GB]:M_COL[GB] + 1]).then_inc(acc_read, 1)

            def silu_table():
                act.preload_act_table(ACT.Silu)

            def first_silu(j):
                silu(j, FIRST_SLOTS[j])

            def weights_hi(group, s, use):
                act.wait_ge(w_loaded[s], 16 * use)
                act.wait_ge(down_done, WG * (group - 2))
                act.activation(w_hi[:, s, :], w_raw[:, s, :], ACT.Copy).then_inc(w_hi_ready, 1)

            def first_hi(j):
                gated_hi(j, j)

            for stage, n in (
                    (bias_hi, None), (modulate_1, 0), (scale_bu, 0), (modulate_1, 1), (scale_bu, 1),
                    (modulate_1, 2), (scale_bu, 2), (normalise_2, 0), (modulate_1, 3), (modulate_2, 0),
                    (normalise_2, 1), (scale_bu, 3), (router_probs, 0), (modulate_2, 1), (normalise_2, 2),
                    (combine_weights, 0), (router_probs, 1), (modulate_2, 2), (keep_combT_a, 0),
                    (keep_combT_b, 0), (normalise_2, 3), (router_probs, 2), (combine_weights, 1),
                    (modulate_2, 3), (shared_sigmoid, None), (keep_combT_a, 1), (keep_combT_b, 1),
                    (router_probs, 3), (combine_weights, 2), (first_hi, 0), (silu_table, None),
                    (first_silu, 1), (first_silu, 2), (keep_combT_a, 2), (first_hi, 1), (first_hi, 2),
                    (first_silu, 3), (keep_combT_b, 2), (first_silu, 4), (combine_weights, 3),
                    (first_hi, 3), (first_silu, 5), (first_hi, 4), (keep_combT_a, 3), (first_silu, 6),
                    (keep_combT_b, 3), (store_combine, 1), (first_hi, 5), (first_silu, 7), (first_hi, 6),
                    (first_silu, 8), (first_hi, 7), (first_hi, 8), (first_silu, 9)):
                stage(n) if n is not None else stage()

            def turn(c, i, last):
                for k in range(BODY):
                    j = PAIRS * c + BODY * i + k
                    if not (last and c == CHUNKS - 1 and k == BODY - 1):
                        silu(j + 1, (k + 1) % RING)
                    gated_hi(j, k)
                    if k % WG == 1 and not (last and c == CHUNKS - 1 and k > 1):
                        s = (k // WG + 2) % RING
                        weights_hi(WGROUPS * c + WG * i + k // WG + 2, s,
                                   WGROUPS // RING * c + i + (1 if s == 2 else 2))
                    if c > 0 and isinstance(i, int) and i == 0 and k == 0:
                        keep_sum(c - 1)

            for c in range(CHUNKS):
                if c > 0:
                    turn(c, 0, False)
                with act.Fori(1, TURNS - 1) as i:
                    turn(c, i, False)
                turn(c, TURNS - 1, True)
            keep_sum(CHUNKS - 1)

        @block.vector
        def _(dve):
            def stats_1(g):
                ln_stats(0, g)

            def stats_2(g):
                ln_stats(1, g)

            def ln_stats(n, g):
                if n == 0:
                    dve.wait_ge(x_loaded[g], 16)
                else:
                    dve.wait_ge(x1_ready, g + 1)
                for t in range(g * GT, (g + 1) * GT):
                    last = dve.bn_stats(bn[:, n, t, :], x_sb[:, t, :])
                last.then_inc(bn_done[n], 1)
                dve.wait_ge(bn_done[n], g + 1)
                for t in range(g * GT, (g + 1) * GT):
                    last = dve.bn_aggr(mv[:, n, t, :], bn[:, n, t, :])
                last.then_inc(mv_done[n], 1)
                dve.wait_ge(mv_done[n], g + 1)
                if n == 1:
                    dve.tensor_scalar(neg_mean[:, tiles(g)], mv[:, n, tiles(g), 0], -1.0, None, ALU.mult)
                dve.tensor_scalar(ve[:, n, tiles(g)], mv[:, n, tiles(g), 1], LN_EPS, None, ALU.add
                                  ).then_inc(var_ready[n], 1)

            def normalise_1(g):
                dve.wait_ge(rstd_ready[0], g + 1)
                for t in range(g * GT, (g + 1) * GT):
                    last = dve.tensor_scalar(xn[:, t, :], x_sb[:, t, :], mv[:, 0, t, 0:1], rstd[:, 0, t:t + 1],
                                             ALU.subtract, ALU.mult)
                last.then_inc(xn_ready[0], 1)

            def silu_columns():
                dve.wait_ge(exps_done, 1)
                dve.tensor_scalar(exp_c1[:, :], exp_c[:, :], 1.0, None, ALU.add).then_inc(siluc_done, 1)
                dve.wait_ge(siluc_done, 1)
                dve.reciprocal(sig_c[:, :], exp_c1[:, :]).then_inc(siluc_done, 1)
                dve.wait_ge(siluc_done, 2)
                dve.tensor_tensor(silu_c[:, :], cols_sb[:, 0:1], sig_c[:, :], ALU.mult).then_inc(siluc_done, 1)
                dve.wait_ge(siluc_done, 3)
                dve.wait_ge(consts_set, 7)
                dve.tensor_scalar(silu_rep[:, :], ones[:, :], silu_c[:, 0:1], None, ALU.mult
                                  ).then_inc(siluc_done, 1)

            def time_step():
                dve.wait_ge(exps_done, 3)
                dve.tensor_tensor(a_dt[:, :], exp_a[:, :], dt_sb[:, :], ALU.mult).then_inc(adt_done, 1)
                dve.tensor_tensor(dt_bias[:, :], cols_sb[:, 2:3], dt_sb[:, :], ALU.mult).then_inc(adt_done, 1)

            def modulation_1():
                dve.wait_ge(mod_product, 1)
                dve.tensor_scalar(ca_p1[:, :], ps[:, B_MOD_1, 1:2], 1.0, None, ALU.add)
                dve.tensor_copy(sa[:, :], ps[:, B_MOD_1, 0:1]).then_inc(mod_1_ready, 1)

            def modulation():
                dve.wait_ge(mod_product, 2)
                dve.tensor_copy(mod[:, :], ps[:, B_MOD, 0:M_ALL])
                dve.tensor_scalar(cb_p1[:, :], ps[:, B_MOD, M_COL[CB]:M_COL[CB] + 1], 1.0, None, ALU.add
                                  ).then_inc(mod_ready, 1)

            def mixer_gate():
                m = ps[:, B_MOD, 0:M_ALL]
                dve.wait_ge(mod_ready, 1)
                dve.scalar_tensor_tensor(out=mod_abs[:, :], in0=m, scalar=-1.0, in1=mod[:, :],
                                         op0=ALU.mult, op1=ALU.max).then_inc(mod_read, 1)
                dve.tensor_scalar(mod_sgn[:, :], m, 0.0, 2.0, ALU.is_ge, ALU.mult).then_inc(mod_read, 1)
                dve.wait_ge(mod_read, 1)
                dve.tensor_scalar(mod_mag[:, :], mod_abs[:, :], GATE_FLOOR, None, ALU.max).then_inc(mod_read, 1)
                dve.wait_ge(mod_read, 3)
                dve.scalar_tensor_tensor(out=mod_gate[:, :], in0=mod_sgn[:, :], scalar=-1.0,
                                         in1=mod_mag[:, :], op0=ALU.add, op1=ALU.mult).then_inc(mod_read, 1)
                dve.wait_ge(rows_loaded, 16)
                dve.tensor_tensor(bias_sum[:, :], rows_sb[:, O_BC:O_BC + H], rows_sb[:, O_BD:O_BD + H],
                                  ALU.add).then_inc(bias_part, 1)
                dve.wait_ge(proj_loaded, 16)
                dve.wait_ge(mod_read, 4)
                ga = mod_gate[:, 0:H]
                dve.tensor_tensor(wc_g[:, :], proj_sb[:, O_WC:O_WC + H], ga, ALU.mult).then_inc(mixer_weights, 1)
                dve.tensor_tensor(wd_g[:, :], proj_sb[:, O_WD:O_WD + H], ga, ALU.mult).then_inc(mixer_weights, 1)
                dve.wait_ge(bias_part, 1)
                dve.tensor_tensor(bias_g[:, :], bias_sum[:, :], ga, ALU.mult).then_inc(mixer_weights, 1)

            def bias_lo():
                dve.wait_ge(bias_hi_done, 1)
                lower = bias_hl[HALF:P, :, :]
                dve.tensor_tensor(lower, expert_bias(HALF, P), lower.bitcast(F32), ALU.subtract
                                  ).then_inc(bias_hl_ready, 1)

            def scan(g):
                if g == 0:
                    dve.wait_ge(abar_done, 1)
                else:
                    dve.wait_ge(states_ready, g)
                dve.wait_ge(bu_ready, g + 1)
                initial = 0.0 if g == 0 else stT[:, g * BANK - 1:g * BANK]
                dve.tensor_tensor_scan(stT[:, tok(g)], a_bar[:, 0:1].to_broadcast((P, BANK)), buT[:, tok(g)],
                                       initial, ALU.mult, ALU.add).then_inc(states_ready, 1)

            def add_mixer(g):
                dve.wait_ge(y_done, g + 1)
                dve.wait_ge(xbias_ready, g + 1)
                dve.tensor_tensor(x_sb[:, tiles(g), :], ps[:, B_Y, :].rearrange("p (q h) -> p q h", q=GT),
                                  x_sb[:, tiles(g), :], ALU.add).then_inc(x1_ready, 1)

            def top_eight(g):
                dve.wait_ge(probs_ready, g + 1)
                for t in range(g * GT, (g + 1) * GT):
                    last = dve.max(top8[:, t, :], probs[:, t, :])
                last.then_inc(top8_done, 1)
                dve.wait_ge(top8_done, g + 1)
                for t in range(g * GT, (g + 1) * GT):
                    last = dve.match_replace(picked[:, t, :], top8[:, t, :], probs[:, t, :], 0.0)
                last.then_inc(rest_ready, 1)
                dve.reduce_sum(top_sum[:, tiles(g)], top8[:, tiles(g), :], AX_X).then_inc(sum_done, 1)
                dve.wait_ge(sum_done, 2 * g + 1)
                dve.tensor_scalar(top_sum_s[:, tiles(g)], top_sum[:, tiles(g)], SUM_EPS, 1.0 / SCALE, ALU.add,
                                  ALU.mult).then_inc(sum_done, 1)
                dve.wait_ge(sum_done, 2 * g + 2)
                dve.reciprocal(top_inv[:, tiles(g)], top_sum_s[:, tiles(g)]).then_inc(inv_ready, 1)

            def select(g):
                dve.wait_ge(rest_ready, g + 1)
                dve.tensor_tensor(picked[:, tiles(g), :], probs[:, tiles(g), :], picked[:, tiles(g), :],
                                  ALU.subtract).then_inc(sel_ready, 1)

            def gate(j, z, k):
                dve.wait_ge(silu_done, j + 1)
                if not (isinstance(j, int) and j < RING):
                    dve.wait_ge(lo_ready, j - RING + 1)
                dve.tensor_tensor(gu[:, k % RING, :].rearrange("p (b n) -> p b n", b=2), slot(z),
                                  cb[:, k % RING, :].rearrange("p (b n) -> p b n", b=2),
                                  ALU.mult).then_inc(gated, 1)

            def gated_lo(j, k):
                dve.wait_ge(hi_ready, j + 1)
                dve.tensor_tensor(g_lo[:, k % RING, :], gu[:, k % RING, :], g_hi[:, k % RING, :].bitcast(F32),
                                  ALU.subtract).then_inc(lo_ready, 1)

            def shared_gate():
                dve.wait_ge(silu_done, 1)
                both = gu[:, 0, :].rearrange("p (b n) -> p b n", b=2)
                dve.tensor_tensor(both, slot(FIRST_SLOTS[0]), both, ALU.mult).then_inc(gated, 1)

            def first_gate(j):
                dve.wait_ge(cb_loaded[j % RING], 16 * (j // RING + (j % RING > 0)))
                gate(j, FIRST_SLOTS[j], j)

            def first_lo(j):
                gated_lo(j, j)

            for stage, n in (
                    (stats_1, 0), (silu_columns, None), (stats_1, 1), (time_step, None), (normalise_1, 0),
                    (modulation_1, None), (stats_1, 2), (normalise_1, 1), (modulation, None),
                    (mixer_gate, None), (scan, 0), (normalise_1, 2), (stats_1, 3), (add_mixer, 0),
                    (scan, 1), (stats_2, 0), (normalise_1, 3), (scan, 2), (add_mixer, 1), (stats_2, 1),
                    (bias_lo, None), (add_mixer, 2), (stats_2, 2), (scan, 3), (top_eight, 0), (select, 0),
                    (add_mixer, 3), (stats_2, 3), (top_eight, 1), (select, 1), (top_eight, 2), (select, 2),
                    (shared_gate, None), (top_eight, 3), (first_lo, 0), (select, 3), (first_gate, 1),
                    (first_gate, 2), (first_lo, 1), (first_lo, 2), (first_gate, 3), (first_gate, 4),
                    (first_lo, 3), (first_gate, 5), (first_lo, 4), (first_gate, 6), (first_lo, 5),
                    (first_gate, 7), (first_lo, 6), (first_gate, 8), (first_lo, 7), (first_lo, 8),
                    (first_gate, 9)):
                stage(n) if n is not None else stage()

            def turn(c, i, last):
                for k in range(BODY):
                    j = PAIRS * c + BODY * i + k
                    if not (last and c == CHUNKS - 1 and k == BODY - 1):
                        ahead = k + 1
                        use = PAIRS // RING * c + BODY // RING * i + ahead // RING + 1
                        dve.wait_ge(cb_loaded[ahead % RING], 16 * (use - (ahead % RING == 0)))
                        gate(j + 1, ahead % RING, ahead)
                    gated_lo(j, k)

            for c in range(CHUNKS):
                if c > 0:
                    turn(c, 0, False)
                with dve.Fori(1, TURNS - 1) as i:
                    turn(c, i, False)
                turn(c, TURNS - 1, True)

            def add_ffn(g, first, end):
                t = slice(g * GT + first, g * GT + end)
                dve.tensor_tensor(out_sb[:, t, :],
                                  ps[:, g, first * P:end * P].rearrange("p (q h) -> p q h", h=H),
                                  x_sb[:, t, :], ALU.add).then_inc(out_ready, 1)

            for g in range(GROUPS):
                if g == GROUPS - GC:
                    dve.wait_ge(down_done, ALL_PAIRS)
                    dve.tensor_scalar(ffT[:, tok(GROUPS - 1)], ps[:, B_ACC + 1, :],
                                      mod_gate[:, M_COL[GB]:M_COL[GB] + 1], None, ALU.mult).then_inc(last_read, 1)
                dve.wait_ge(ffn_turned, g + 1)
                if g == GROUPS - 1:
                    add_ffn(g, 0, GT // 2)
                    add_ffn(g, GT // 2, GT)
                else:
                    add_ffn(g, 0, GT)

        @block.tensor
        def _(pe):
            pe.wait_ge(consts_set, 7)
            for _ in range(WARM_UP):
                pe.matmul(ps[:, B_MOD, :], zeros_r[:, :],
                          zeros_r[:, :].rearrange("p (a n) -> p a n", a=1).to_broadcast((P, GT, P)),
                          start=True, stop=True)

            def modulation():
                pe.wait_ge(wmod_loaded, 16)
                pe.wait_ge(siluc_done, 3)
                for n, m in enumerate((SA, CA)):
                    last = pe.matmul(ps[:, B_MOD_1, n:n + 1], wmod_sb[:, m * H:(m + 1) * H], silu_c[:, :],
                                     start=True, stop=True)
                last.then_inc(mod_product, 1)
                pe.wait_ge(siluc_done, 4)
                pe.matmul(ps[:, B_MOD, 0:H], silu_rep[:, :], wmod_sb[:, GA * H:(GA + 1) * H], start=True, stop=True)
                for m in AS_COLUMN:
                    last = pe.matmul(ps[:, B_MOD, M_COL[m]:M_COL[m] + 1], wmod_sb[:, m * H:(m + 1) * H],
                                     silu_c[:, :], start=True, stop=True)
                last.then_inc(mod_product, 1)

            def turn_1(g):
                turn_tokens(0, g)

            def turn_2(g):
                turn_tokens(1, g)

            def turn_tokens(n, g):
                if n == 0 and g == 0:
                    pe.wait_ge(ident_set, 1)
                pe.wait_ge(xn_ready[n], g + 1)
                if g > 0:
                    pe.wait_ge(h2T_ready if n else hT_ready, g)
                for q in range(GT):
                    last = pe.transpose(ps[:, B_H2T if n else B_XT, q * P:(q + 1) * P], xn[:, g * GT + q, :],
                                        ident[:, :])
                last.then_inc(xT_done[n], 1)

            def project_b(g):
                if g == 0:
                    pe.wait_ge(proj_loaded, 16)
                pe.wait_ge(hT_ready, g + 1)
                if g > 0:
                    pe.wait_ge(bu_ready, g)
                pe.matmul(ps[:, B_BU, :], proj_sb[:, O_WB:O_WB + P], hT[:, tok(g)], start=True, stop=True
                          ).then_inc(bu_done, 1)

            def project_y(g):
                if g == 0:
                    pe.wait_ge(mixer_weights, 2)
                else:
                    pe.wait_ge(x1_ready, g)
                pe.wait_ge(states_ready, g + 1)
                for q in range(GT):
                    cols = slice(g * BANK + q * P, g * BANK + (q + 1) * P)
                    dst = ps[:, B_Y, q * P:(q + 1) * P]
                    pe.matmul(dst, hT[:, cols], wd_g[:, :], start=True, stop=False)
                    last = pe.matmul(dst, stT[:, cols], wc_g[:, :], start=False, stop=True)
                last.then_inc(y_done, 1)

            def route(g):
                if g == 0:
                    pe.wait_ge(proj_loaded, 16)
                    pe.wait_ge(bias_hl_ready, 1)
                else:
                    pe.wait_ge(probs_ready, g)
                pe.wait_ge(h2T_ready, g + 1)
                for b in range(GT // 2):
                    pe.matmul(ps[:, B_LOGIT + b, 0:2 * NE], share_r[:, :],
                              bias_hl[:, :, :].rearrange("p a e -> p (a e)"), start=True, stop=False)
                    for q in range(2):
                        t = 2 * b + q
                        last = pe.matmul(ps[:, B_LOGIT + b, q * NE:(q + 1) * NE],
                                         h2T[:, g * BANK + t * P:g * BANK + (t + 1) * P],
                                         proj_sb[:, O_RT:O_RT + NE], start=False, stop=(q == 1))
                last.then_inc(logits_done, 1)

            def turn_combine(g):
                pe.wait_ge(comb_ready, g + 1)
                if g > 0:
                    pe.wait_ge(combT_a_ready, g)
                    pe.wait_ge(combT_b_ready, g)
                if B_COMBT[g] == B_LOGIT:
                    pe.wait_ge(probs_ready, GROUPS)
                if g == 0:
                    pe.wait_ge(mod_read, 3)
                    pe.wait_ge(mod_1_ready, 1)
                for q in range(GT):
                    t = g * GT + q
                    pe.transpose(ps[:, B_COMBT[g], q * P:(q + 1) * P], comb[:, t, 0:P], ident[:, :])
                    last = pe.transpose(ps[0:EC - P, B_COMBT[g] + 1, q * P:(q + 1) * P], comb[:, t, P:EC],
                                        ident[:, :])
                last.then_inc(combT_done, 1)

            def inner(chunk, z, k):
                cols = slice(k % WG * P, (k % WG + 1) * P)
                hi, lo = w_hi[:, k // WG % RING, cols], w_lo[:, k // WG % RING, cols]
                for n, (w, v) in enumerate(((hi, h2_hi), (hi, h2_lo), (lo, h2_hi))):
                    for b in range(2):
                        last = pe.matmul(ps[:, 2 * z + b, :], w,
                                         v[:, chunk * CHUNK + b * BANK:chunk * CHUNK + (b + 1) * BANK],
                                         start=(n == 0), stop=(n == 2))
                last.then_inc(z_ready, 1)

            def down(j, k, end):
                base = WG * P + k % WG * P
                hi = w_hi[:, k // WG % RING, base:base + P]
                lo = w_lo[:, k // WG % RING, base:base + P]
                pe.wait_ge(hi_ready, j + 1)
                for n, (w, v) in enumerate(((hi, g_hi), (lo, g_hi), (hi, g_lo))):
                    if n == 2:
                        pe.wait_ge(lo_ready, j + 1)
                    for b in range(2):
                        last = pe.matmul(ps[:, B_ACC + b, :], w, v[:, k % RING, b * BANK:(b + 1) * BANK],
                                         start=False, stop=(end and n == 2))
                        if n == 2 and b == 0 and isinstance(j, int) and j == ALL_PAIRS - 1:
                            last.then_inc(half_summed, 1)
                last.then_inc(down_done, 1)

            def clear_acc(c):
                if c == 0:
                    pe.wait_ge(combT_a_ready, GC)
                    pe.wait_ge(combT_b_ready, GC)
                else:
                    pe.wait_ge(acc_read, 2 * c)
                for b in range(2):
                    pe.matmul(ps[:, B_ACC + b, :], zeros_r[:, :], h2_hi[:, b * BANK:(b + 1) * BANK],
                              start=True, stop=False)

            def first_inner(j):
                z = FIRST_SLOTS[j]
                users = [p for p in range(j) if FIRST_SLOTS[p] == z]
                if users:
                    pe.wait_ge(gated, users[-1] + 1)
                elif z == 0:
                    pe.wait_ge(hT_ready, GROUPS)
                    pe.wait_ge(bu_ready, GROUPS)
                elif z == 1:
                    pe.wait_ge(x1_ready, GROUPS)
                    pe.wait_ge(h2T_ready, GROUPS)
                else:
                    pe.wait_ge(combT_a_ready, GROUPS)
                    pe.wait_ge(combT_b_ready, GROUPS)
                if j == 0:
                    pe.wait_ge(h2_lo_ready, GC)
                if j % WG == 0:
                    pe.wait_ge(w_split, j // WG + 1)
                inner(0, z, j)

            def first_down(j):
                down(j, j, False)

            for stage, n in (
                    (modulation, None), (turn_1, 0), (project_b, 0), (turn_1, 1), (project_b, 1),
                    (project_y, 0), (turn_1, 2), (project_b, 2), (project_y, 1), (turn_1, 3),
                    (project_y, 2), (turn_2, 0), (project_b, 3), (route, 0), (turn_2, 1), (project_y, 3),
                    (route, 1), (turn_2, 2), (turn_combine, 0), (route, 2), (first_inner, 0), (turn_2, 3),
                    (turn_combine, 1), (route, 3), (first_inner, 1), (first_inner, 2), (turn_combine, 2),
                    (clear_acc, 0), (first_down, 0), (first_inner, 3), (first_inner, 4), (first_down, 1),
                    (first_down, 2), (first_inner, 5), (turn_combine, 3), (first_inner, 6),
                    (first_down, 3), (first_inner, 7), (first_inner, 8), (first_inner, 9), (first_down, 4),
                    (first_down, 5), (first_inner, 10), (first_down, 6), (first_down, 7),
                    (first_inner, 11), (first_down, 8)):
                stage(n) if n is not None else stage()

            def next_inner(c, i, k, last):
                ahead = k + LEAD
                chunk = c
                if last and ahead >= BODY:
                    if c == CHUNKS - 1:
                        return
                    chunk = c + 1
                j = PAIRS * c + BODY * i + k
                pe.wait_ge(gated, j + 1)
                if ahead % WG == 0:
                    pe.wait_ge(w_split, WGROUPS * c + WG * i + ahead // WG + 1)
                inner(chunk, ahead % RING, ahead)

            def turn_ffn(c, z):
                for t in range(CHUNK // P):
                    if t % GT == 0 and c == CHUNKS - 1 and t > 0:
                        pe.wait_ge(last_read, 1)
                    elif t % GT == 0:
                        pe.wait_ge(acc_read, 2 * c + t // GT + 1)
                    last = pe.transpose(ps[:, 2 * z + t // GT, t % GT * P:(t % GT + 1) * P],
                                        ffT[:, c * CHUNK + t * P:c * CHUNK + (t + 1) * P], ident[:, :])
                    if t % GT == GT - 1:
                        last.then_inc(ffn_turned, 1)

            def turn(c, i, last):
                for k in range(BODY):
                    next_inner(c, i, k, last)
                    if c > 0 and isinstance(i, int) and i == 0 and k == 0:
                        clear_acc(c)
                    if last and c == CHUNKS - 1 and k == BODY - 2:
                        turn_ffn(0, 0)
                    down(PAIRS * c + BODY * i + k, k, last and k == BODY - 1)

            for c in range(CHUNKS):
                if c > 0:
                    turn(c, 0, False)
                with pe.Fori(1, TURNS - 1) as i:
                    turn(c, i, False)
                if c == 0:
                    pe.wait_ge(h2_lo_ready, GROUPS)
                turn(c, TURNS - 1, True)
            for c in range(1, CHUNKS):
                turn_ffn(c, c)


def kernel(L0_attn_u, L0_attn_log_A, L0_attn_W_B, L0_attn_b_B, L0_attn_W_C, L0_attn_b_C, L0_attn_W_D, L0_attn_b_D,
           L0_attn_log_dt, L0_ffn_router_w, L0_ffn_expert_bias, L0_ffn_w_gate, L0_ffn_w_down,
           L0_ffn_w_gate_shared, L0_ffn_w_down_shared, L0_c, L0_wmod):
    import numpy as np
    import concourse.bacc as bacc
    from concourse.bass_utils import run_bass_kernel_spmd

    def arr(a):
        return np.asarray(a)

    gate = np.concatenate([arr(L0_ffn_w_gate_shared)[None], np.zeros((1, INTER, H), np.float32),
                           arr(L0_ffn_w_gate)])
    down = np.concatenate([arr(L0_ffn_w_down_shared)[None], np.zeros((1, H, INTER), np.float32),
                           arr(L0_ffn_w_down)])
    gate = gate.reshape(WGROUPS, WG, P, H).transpose(0, 3, 1, 2).reshape(WGROUPS, P, WG * P)
    down = down.transpose(0, 2, 1).reshape(WGROUPS, WG, P, H).transpose(0, 2, 1, 3).reshape(WGROUPS, P, WG * P)
    arrays = {
        "x": arr(L0_attn_u),
        "columns": np.stack([arr(L0_c)[0], arr(L0_attn_log_A), arr(L0_attn_b_B)], axis=1),
        "log_dt": arr(L0_attn_log_dt).reshape(1, 1),
        "rows": np.concatenate([arr(L0_attn_b_C), arr(L0_attn_b_D), arr(L0_ffn_expert_bias)])[None],
        "wmod": arr(L0_wmod),
        "proj": np.concatenate([arr(L0_attn_W_B).T, arr(L0_attn_W_C).T, arr(L0_attn_W_D).T,
                                arr(L0_ffn_router_w).T], axis=1),
        "experts": np.concatenate([gate, down], axis=2),
    }
    arrays = {n: np.ascontiguousarray(a) for n, a in arrays.items()}
    nc = bacc.Bacc("TRN2", target_bir_lowering=False, num_devices=1)
    args = [nc.dram_tensor(n, a.shape, F32, kind="ExternalInput").ap() for n, a in arrays.items()]
    out = nc.dram_tensor("out", (1, T, H), F32, kind="ExternalOutput").ap()
    adaln_layer(nc, *args, out)
    r = run_bass_kernel_spmd(nc, [arrays], core_ids=[0])
    return r.results[0]["out"]
```
